# Optimizing a Trainium2 kernel written in Bass

```python
import numpy as np
import jax
import jax.numpy as jnp

def _softmax(x, axis=-1):
    return jax.nn.softmax(x, axis=axis)

def _gelu(x):
    return jax.nn.gelu(x, approximate=True)

def _silu(x):
    return jax.nn.silu(x)

def _sigmoid(x):
    return jax.nn.sigmoid(x)

def _layernorm(x, axis=-1, eps=1e-05):
    m = jnp.mean(x, axis=axis, keepdims=True)
    v = jnp.var(x, axis=axis, keepdims=True)
    return (x - m) / jnp.sqrt(v + eps)

def _scatter_add(tgt, idx, src, axis=0):
    return tgt.at[idx].add(src)

def _segment_sum(src, seg, n):
    return jax.ops.segment_sum(src, seg, n)
kernel_name = 'mk_gnn_preln_d2_gnn_r8_78eeea'

def setup_inputs(seed: int=0):
    np.random.seed(seed)
    _w = jnp.asarray

    def _rec_inputs():
        import jax
        import jax.numpy as jnp
        _gk = jax.random.key(seed)
        x = -0.0001006 + 1 * jax.random.normal(jax.random.fold_in(_gk, 1), (6250, 96), jnp.float32)
        _s = jax.random.randint(jax.random.fold_in(_gk, 2), (100000,), 0, 6250, jnp.int32)
        _d = jax.random.randint(jax.random.fold_in(_gk, 3), (100000,), 0, 6250, jnp.int32)
        _loop = jnp.arange(6250, dtype=jnp.int32)
        src = jnp.concatenate([_s, _d, _loop])
        dst = jnp.concatenate([_d, _s, _loop])
        _o = jnp.argsort(dst, stable=True)
        src = src[_o]
        dst = dst[_o]
        edge_attr_32 = 0.000196303 + 1.00016 * jax.random.normal(jax.random.fold_in(_gk, 12), (206250, 32), jnp.float32)
        return (x, src, dst, edge_attr_32)
    x, src, dst, edge_attr_32 = _rec_inputs()

    def _L0_gnn_setup():
        import jax, jax.numpy as jnp
        import numpy as np
        N, E = (6250, 100000)
        DIN = DOUT = 96
        DE = 32

        def _egnn_conv(x, src, dst, edge_attr, W_msg, W_edge, W_root, b):
            msg = x[src] @ W_msg + edge_attr @ W_edge
            agg = jax.ops.segment_max(msg, dst, num_segments=x.shape[0])
            agg = jnp.where(jnp.isneginf(agg), 0.0, agg)
            return agg + x @ W_root + b
        key = jax.random.key(seed)
        ks = jax.random.split(key, 10)
        rn = lambda k, sh, sc: jax.random.normal(k, sh, jnp.float32) * sc
        return {'X': rn(ks[0], (N, DIN), 1.0), 'edge_index': jax.random.randint(ks[1], (2, E), 0, N, jnp.int32), 'edge_attr': rn(ks[2], (E, DE), 1.0), 'W1_msg': rn(ks[3], (DIN, DOUT), DIN ** (-0.5)), 'W1_edge': rn(ks[4], (DE, DOUT), DE ** (-0.5)), 'W1_root': rn(ks[5], (DIN, DOUT), DIN ** (-0.5)), 'b1': jnp.zeros((DOUT,), jnp.float32), 'W2_msg': rn(ks[6], (DOUT, DOUT), DOUT ** (-0.5)), 'W2_edge': rn(ks[7], (DE, DOUT), DE ** (-0.5)), 'W2_root': rn(ks[8], (DOUT, DOUT), DOUT ** (-0.5)), 'b2': jnp.zeros((DOUT,), jnp.float32)}
    _L0_gnn_all = _L0_gnn_setup()
    _L0_gnn_in = {k: v for k, v in _L0_gnn_all.items() if k in ('W1_msg', 'W1_edge', 'W1_root', 'b1', 'W2_msg', 'W2_edge', 'W2_root', 'b2')}
    del _L0_gnn_all

    def _L1_gnn_setup():
        import jax, jax.numpy as jnp
        import numpy as np
        N_NODES = 6250
        N_EDGES = 100000
        D_IN = 96
        D_HID = 96
        D_OUT = 96

        def _mean_agg(x, src, dst, n_nodes):
            msg = x[src]
            summed = jax.ops.segment_sum(msg, dst, num_segments=n_nodes)
            deg = jax.ops.segment_sum(jnp.ones((src.shape[0],), x.dtype), dst, num_segments=n_nodes)
            return summed / jnp.maximum(deg, 1.0)[:, None]

        def _sage_conv(x, src, dst, W_self, W_neigh, b):
            agg = _mean_agg(x, src, dst, x.shape[0])
            return x @ W_self + agg @ W_neigh + b
        key = jax.random.key(seed)
        ks = jax.random.split(key, 9)
        s = 0.05
        return {'x': jax.random.normal(ks[0], (N_NODES, D_IN), jnp.float32), 'src': jax.random.randint(ks[1], (N_EDGES,), 0, N_NODES), 'dst': jax.random.randint(ks[2], (N_EDGES,), 0, N_NODES), 'W_self1': jax.random.normal(ks[3], (D_IN, D_HID), jnp.float32) * s, 'W_neigh1': jax.random.normal(ks[4], (D_IN, D_HID), jnp.float32) * s, 'b1': jnp.zeros((D_HID,), jnp.float32), 'W_self2': jax.random.normal(ks[5], (D_HID, D_OUT), jnp.float32) * s, 'W_neigh2': jax.random.normal(ks[6], (D_HID, D_OUT), jnp.float32) * s, 'b2': jnp.zeros((D_OUT,), jnp.float32)}
    _L1_gnn_all = _L1_gnn_setup()
    _L1_gnn_in = {k: v for k, v in _L1_gnn_all.items() if k in ('W_self1', 'W_neigh1', 'b1', 'W_self2', 'W_neigh2', 'b2')}
    del _L1_gnn_all
    return {'x': x, 'src': src, 'dst': dst, 'edge_attr_32': edge_attr_32, 'L0_gnn_W1_msg': _L0_gnn_in['W1_msg'], 'L0_gnn_W1_edge': _L0_gnn_in['W1_edge'], 'L0_gnn_W1_root': _L0_gnn_in['W1_root'], 'L0_gnn_b1': _L0_gnn_in['b1'], 'L0_gnn_W2_msg': _L0_gnn_in['W2_msg'], 'L0_gnn_W2_edge': _L0_gnn_in['W2_edge'], 'L0_gnn_W2_root': _L0_gnn_in['W2_root'], 'L0_gnn_b2': _L0_gnn_in['b2'], 'L1_gnn_W_self1': _L1_gnn_in['W_self1'], 'L1_gnn_W_neigh1': _L1_gnn_in['W_neigh1'], 'L1_gnn_b1': _L1_gnn_in['b1'], 'L1_gnn_W_self2': _L1_gnn_in['W_self2'], 'L1_gnn_W_neigh2': _L1_gnn_in['W_neigh2'], 'L1_gnn_b2': _L1_gnn_in['b2']}

def reference(x, src, dst, edge_attr_32, L0_gnn_W1_msg, L0_gnn_W1_edge, L0_gnn_W1_root, L0_gnn_b1, L0_gnn_W2_msg, L0_gnn_W2_edge, L0_gnn_W2_root, L0_gnn_b2, L1_gnn_W_self1, L1_gnn_W_neigh1, L1_gnn_b1, L1_gnn_W_self2, L1_gnn_W_neigh2, L1_gnn_b2):
    import jax
    import jax.numpy as jnp

    def _L0_gnn_ref(X, edge_index, edge_attr, W1_msg, W1_edge, W1_root, b1, W2_msg, W2_edge, W2_root, b2):
        import jax, jax.numpy as jnp
        import numpy as np
        N, E = (6250, 100000)
        DIN = DOUT = 96
        DE = 32

        def _egnn_conv(x, src, dst, edge_attr, W_msg, W_edge, W_root, b):
            msg = x[src] @ W_msg + edge_attr @ W_edge
            agg = jax.ops.segment_max(msg, dst, num_segments=x.shape[0])
            agg = jnp.where(jnp.isneginf(agg), 0.0, agg)
            return agg + x @ W_root + b
        src, dst = (edge_index[0], edge_index[1])
        c1 = jax.nn.leaky_relu(_egnn_conv(X, src, dst, edge_attr, W1_msg, W1_edge, W1_root, b1))
        c2 = jax.nn.leaky_relu(_egnn_conv(c1, src, dst, edge_attr, W2_msg, W2_edge, W2_root, b2))
        return c2

    def _L1_gnn_ref(x, src, dst, W_self1, W_neigh1, b1, W_self2, W_neigh2, b2):
        import jax, jax.numpy as jnp
        import numpy as np
        N_NODES = 6250
        N_EDGES = 100000
        D_IN = 96
        D_HID = 96
        D_OUT = 96

        def _mean_agg(x, src, dst, n_nodes):
            msg = x[src]
            summed = jax.ops.segment_sum(msg, dst, num_segments=n_nodes)
            deg = jax.ops.segment_sum(jnp.ones((src.shape[0],), x.dtype), dst, num_segments=n_nodes)
            return summed / jnp.maximum(deg, 1.0)[:, None]

        def _sage_conv(x, src, dst, W_self, W_neigh, b):
            agg = _mean_agg(x, src, dst, x.shape[0])
            return x @ W_self + agg @ W_neigh + b
        h = _sage_conv(x, src, dst, W_self1, W_neigh1, b1)
        h = jax.nn.relu(h)
        h = _sage_conv(h, src, dst, W_self2, W_neigh2, b2)
        return h
    edge_index = jnp.stack([src, dst])
    h = jnp.maximum(_layernorm(x, axis=-1), 0.0)
    x = x + _L0_gnn_ref(h, edge_index, edge_attr_32, L0_gnn_W1_msg, L0_gnn_W1_edge, L0_gnn_W1_root, L0_gnn_b1, L0_gnn_W2_msg, L0_gnn_W2_edge, L0_gnn_W2_root, L0_gnn_b2)
    h = jnp.maximum(_layernorm(x, axis=-1), 0.0)
    x = x + _L1_gnn_ref(h, src, dst, L1_gnn_W_self1, L1_gnn_W_neigh1, L1_gnn_b1, L1_gnn_W_self2, L1_gnn_W_neigh2, L1_gnn_b2)
    return x

_drawn_inputs = setup_inputs


def setup_inputs(seed=0):
    import zlib

    import numpy as np

    out = dict(_drawn_inputs(seed))
    spreads = {'L0_gnn_b1': (0.0, 0.305),
     'L0_gnn_b2': (0.0, 0.444),
     'L1_gnn_b1': (0.0, 0.8),
     'L1_gnn_b2': (0.0, 0.308)}
    factors = {}
    for name, (base, spread) in spreads.items():
        noise = np.random.default_rng([zlib.crc32(name.encode()), seed]).standard_normal(out[name].shape)
        drawn = base * np.exp(spread * noise) if base else spread * noise
        out[name] = jnp.asarray(drawn.astype(out[name].dtype))
    for name, factor in factors.items():
        out[name] = (out[name] * factor).astype(out[name].dtype)
    return out
```

```python
import concourse.bass as bass
from concourse import mybir
from contextlib import ExitStack

N = 6250
D = 96
DA = 32
E = 206250
P = 128
CHUNK = P
CPG = 4
GROUP = CPG * CHUNK
GPI = 4
TURN = GPI * GROUP
TURNS = -(-E // TURN)
EP = TURNS * TURN
CHUNKS = EP // CHUNK
GROUPS = EP // GROUP
B = 10
H = B // 2
NT = -(-N // (B * P)) * B
NTURNS = NT // B
FULL = N // P
REST = N - FULL * P
ZROW = EP
BIG = 3.3895313892515355e38
EPS = 1e-5
CONVS = 4
MAXC = (0, 1)


def gnn_kernel(nc: bass.Bass, x, src_t, dst_t, dst_line, attr_t,
               w_msg1, w_edge1, w_root1, b1, w_msg2, w_edge2, w_root2, b2,
               s_self1, s_neigh1, sb1, s_self2, s_neigh2, sb2, out):
    fp32 = mybir.dt.float32
    bf16 = mybir.dt.bfloat16
    i32 = mybir.dt.int32
    u32 = mybir.dt.uint32
    ALU = mybir.AluOpType
    ACT = mybir.ActivationFunctionType
    ds = bass.ds

    table = nc.dram_tensor("table", (NT * P, D), fp32, kind="Internal").ap()
    scanned_rows = nc.dram_tensor("scanned_rows", (EP + 6, D), fp32, kind="Internal").ap()
    masks = nc.dram_tensor("masks", (2, EP), bf16, kind="Internal").ap()

    ctx = ExitStack()
    with ctx:
        def sb(name, shape, dt=fp32):
            return ctx.enter_context(nc.sbuf_tensor(name, shape, dt))

        def pb(name, shape, dt=fp32):
            return ctx.enter_context(nc.psum_tensor(name, shape, dt))

        def sem(name):
            return ctx.enter_context(nc.semaphore(name))

        ident = sb("ident", [P, P])
        tri = sb("tri", [P, P])
        ones = sb("ones", [P, P])
        iota_i = sb("iota_i", [P, P], i32)
        iota_b = sb("iota_b", [P, P], bf16)
        zbf = sb("zbf", [P, P], bf16)
        zrow = sb("zrow", [1, D])
        w_cat = [sb(f"w_cat{c}", [D, 2 * D]) for c in range(CONVS)]
        w_edge = [sb(f"w_edge{c}", [P, GPI, D]) for c in MAXC]
        bias = [sb(f"bias{c}", [P, D]) for c in range(CONVS)]
        src_i = sb("src_i", [P, CHUNKS], i32)
        dst_i = sb("dst_i", [P, CHUNKS], i32)
        line = sb("line", [P, CHUNKS], i32)
        prev = sb("prev", [P, CHUNKS], i32)
        hi_b = sb("hi_b", [P, CHUNKS], bf16)
        lo_b = sb("lo_b", [P, CHUNKS], bf16)
        mask_max = sb("mask_max", [P, CHUNKS], bf16)
        mask_sum = sb("mask_sum", [P, CHUNKS], bf16)
        hot_lo = sb("hot_lo", [P, GPI * CPG, P], bf16)
        hot_hi = sb("hot_hi", [P, GPI * CPG, NT], bf16)
        idx = sb("idx", [P, GPI, CPG], i32)
        rows = sb("rows", [P, GPI, CPG, D])
        attr = sb("attr", [P, GROUP])
        mask = sb("mask", [D, GPI, GROUP], bf16)
        scan = sb("scan", [D, GPI, GROUP])
        back = sb("back", [P, GPI, CPG * D])
        xs = sb("xs", [P, NT, D])
        root = sb("root", [P, NT, D])
        y = sb("y", [P, NT, D])
        deg = sb("deg", [P, NT])
        nonzero = sb("nonzero", [P, NT])
        inv_deg = sb("inv_deg", [P, NT])
        tot = sb("tot", [P, NT])
        pre = sb("pre", [P, NT])
        endf = sb("endf", [P, NT])
        end_i = sb("end_i", [P, NT], i32)
        part = sb("part", [P, NT], i32)
        part2 = sb("part2", [P, NT], i32)
        end_row = sb("end_row", [P, NT], i32)
        end_idx = sb("end_idx", [P, B], i32)
        agg = sb("agg", [P, B, D])
        feat = sb("feat", [P, B, D])
        tmp = sb("tmp", [P, D])
        stats = sb("stats", [P, 6])
        mv = sb("mv", [P, 2])
        std = sb("std", [P, 1])
        rstd = sb("rstd", [P, 1])
        featT = sb("featT", [D, 2, P])
        msg = sb("msg", [P, B, D])
        epsc = sb("epsc", [P, 1])

        ps_msg = [pb(f"ps_msg{g}", [P, GROUP]) for g in range(GPI)]
        ps_back = [pb(f"ps_back{g}", [P, GROUP]) for g in range(2)]
        ps_deg = pb("ps_deg", [P, GROUP])
        ps_cum = pb("ps_cum", [P, GROUP])

        weights_in = sem("weights_in")
        edges_in = sem("edges_in")
        nodes_in = sem("nodes_in")
        zeroed = sem("zeroed")
        masks_made = sem("masks_made")
        masks_stored = sem("masks_stored")
        pool_const = sem("pool_const")
        dve_step = sem("dve_step")
        hot_made = sem("hot_made")
        hot_used = sem("hot_used")
        deg_made = sem("deg_made")
        deg_copied = sem("deg_copied")
        cum_made = sem("cum_made")
        end_rows_made = sem("end_rows_made")
        idx_staged = sem("idx_staged")
        gathered = [sem(f"gathered{g}") for g in range(GPI)]
        attr_in = sem("attr_in")
        mask_in = [sem(f"mask_in{g}") for g in range(GPI)]
        msgs_made = sem("msgs_made")
        scan_done = sem("scan_done")
        back_made = sem("back_made")
        back_copied = sem("back_copied")
        back_stored = [sem(f"back_stored{g}") for g in range(GPI)]
        end_staged = sem("end_staged")
        agg_in = [sem(f"agg_in{h}") for h in range(2)]
        feat_made = sem("feat_made")
        feat_turned = sem("feat_turned")
        featT_copied = sem("featT_copied")
        prod_made = sem("prod_made")
        msg_copied = sem("msg_copied")
        root_made = sem("root_made")
        table_stored = [sem(f"table_stored{h}") for h in range(2)]
        pool_passed = sem("pool_passed")
        dve_passed = sem("dve_passed")
        std_made = sem("std_made")
        var_made = sem("var_made")
        out_made = sem("out_made")
        out_stored = sem("out_stored")

        block = ctx.enter_context(nc.Block())

        W_DMAS = 2 * CONVS + GPI * len(MAXC) + CONVS

        @block.sync
        def _(sp):
            sp.wait_ge(zeroed, 1)
            sp.dma_start(xs[:, 0:FULL, :], x[0:FULL * P, :].rearrange("(t p) d -> p t d", p=P)).then_inc(nodes_in, 16)
            sp.dma_start(xs[0:REST, FULL, :], x[FULL * P:N, :]).then_inc(nodes_in, 16)
            sp.dma_start(line[:, :], dst_line[1:1 + EP].rearrange("(p c) -> p c", p=P)).then_inc(edges_in, 16)
            sp.dma_start(prev[:, :], dst_line[0:EP].rearrange("(p c) -> p c", p=P)).then_inc(edges_in, 16)
            sp.dma_start(src_i[:, :], src_t).then_inc(edges_in, 16)
            sp.dma_start(dst_i[:, :], dst_t).then_inc(edges_in, 16)
            for c, (wm, wr, b) in enumerate([(w_msg1, w_root1, b1), (w_msg2, w_root2, b2),
                                             (s_neigh1, s_self1, sb1), (s_neigh2, s_self2, sb2)]):
                sp.dma_start(w_cat[c][:, 0:D], wm).then_inc(weights_in, 16)
                sp.dma_start(w_cat[c][:, D:2 * D], wr).then_inc(weights_in, 16)
                sp.dma_start(bias[c][:, :], b.rearrange("(a d) -> a d", a=1).to_broadcast([P, D])).then_inc(weights_in, 16)
            for c, we in enumerate([w_edge1, w_edge2]):
                for g in range(GPI):
                    sp.dma_start(w_edge[c][DA * g:DA * g + DA, g, :], we).then_inc(weights_in, 16)
            for j, stored in enumerate(back_stored + table_stored):
                sp.dma_start(scanned_rows[ZROW + j:ZROW + j + 1, :], zrow[0:1, :]).then_inc(stored, 16)
            sp.wait_ge(masks_made, 1)
            sp.dma_start(masks[0, :].rearrange("(p c) -> p c", p=P), mask_max[:, :]).then_inc(masks_stored, 16)
            sp.dma_start(masks[1, :].rearrange("(p c) -> p c", p=P), mask_sum[:, :]).then_inc(masks_stored, 16)
            sp.wait_ge(masks_stored, 32)
            for c in range(CONVS):
                with sp.Fori(0, NTURNS) as i:
                    for h in range(2):
                        sp.wait_ge(msg_copied, (i + c * NTURNS) * B + (h + 1) * H + 2)
                        sp.dma_start(
                            table[ds(i * (B * P) + h * H * P, H * P), :].rearrange("(t p) d -> p t d", p=P),
                            msg[:, h * H:(h + 1) * H, :]).then_inc(table_stored[h], 16)
                with sp.Fori(0, TURNS) as i:
                    for g in range(GPI):
                        if g == 0 and c in MAXC:
                            sp.wait_ge(msgs_made, i * GPI + c * GROUPS + GPI)
                            sp.dma_start(attr[:, :], attr_t[ds(i * P, P), :]).then_inc(attr_in, 16)
                        sp.wait_ge(scan_done, i * GPI + c * GROUPS + g + 1)
                        m = masks[0 if c in MAXC else 1, ds(i * TURN + g * GROUP, GROUP)]
                        sp.dma_start(mask[:, g, :], m.rearrange("(a e) -> a e", a=1).to_broadcast([D, GROUP])).then_inc(mask_in[g], 16)
            sp.wait_ge(out_made, 1)
            sp.dma_start(out[0:FULL * P, :].rearrange("(t p) d -> p t d", p=P), y[:, 0:FULL, :]).then_inc(out_stored, 16)
            sp.dma_start(out[FULL * P:N, :], y[0:REST, FULL, :]).then_inc(out_stored, 16)
            sp.wait_ge(out_stored, 32)

        @block.gpsimd
        def _(pool):
            pool.memset(xs[:, FULL:NT, :], 0.0)
            pool.memset(zrow[:, :], 0.0)
            pool.memset(w_edge[0][:, :, :], 0.0)
            pool.memset(w_edge[1][:, :, :], 0.0)
            pool.memset(scan[:, :, :], 0.0).then_inc(zeroed, 1)
            pool.memset(zbf[:, :], 0.0)
            pool.memset(epsc[:, :], EPS)
            pool.memset(ones[:, :], 1.0)
            pool.memset(ident[:, :], 0.0).then_inc(pool_const, 1)
            pool.wait_ge(pool_const, 1)
            pool.affine_select(out=ident[:, :], in_=ident[:, :], compare_op=ALU.not_equal, fill=1.0,
                               base=0, pattern=[[-1, P]], channel_multiplier=1)
            pool.affine_select(out=tri[:, :], in_=ones[:, :], compare_op=ALU.is_ge, fill=0.0,
                               base=0, pattern=[[1, P]], channel_multiplier=-1)
            pool.iota(iota_i[:, :], pattern=[[1, P]], base=0, channel_multiplier=0).then_inc(pool_const, 1)
            for c in range(CONVS):
                pool.wait_ge(table_stored[0], 16 * NTURNS * (c + 1) + 16)
                pool.wait_ge(table_stored[1], 16 * NTURNS * (c + 1) + 16)
                with pool.Fori(0, TURNS) as i:
                    for g in range(GPI):
                        n = i * GPI + c * GROUPS + g
                        pool.wait_ge(idx_staged, n + 1)
                        pool.wait_ge(msgs_made, n + 1)
                        pool.sem_inc(pool_passed, 1)
                        for k in range(CPG):
                            pool.indirect_dma_start(
                                rows[:, g, k, :], None, table,
                                bass.IndirectOffsetOnAxis(ap=idx[:, g, k:k + 1], axis=0)).then_inc(gathered[g], 16)
                for g in range(GPI):
                    pool.wait_ge(back_stored[g], 16 * TURNS * (c + 1) + 16)
                if c == 0:
                    pool.wait_ge(end_rows_made, 1)
                with pool.Fori(0, NTURNS) as i:
                    for h in range(2):
                        for s in range(h * H, (h + 1) * H):
                            n = (i + c * NTURNS) * B + s
                            pool.wait_ge(feat_made, n + NT + 1)
                            pool.tensor_copy(end_idx[:, s:s + 1], end_row[:, ds(i * B + s, 1)]).then_inc(end_staged, 1)
                            pool.wait_ge(end_staged, n + 1)
                            pool.sem_inc(pool_passed, 1)
                            pool.indirect_dma_start(
                                agg[:, s, :], None, scanned_rows,
                                bass.IndirectOffsetOnAxis(ap=end_idx[:, s:s + 1], axis=0)).then_inc(agg_in[h], 16)

        @block.scalar
        def _(act):
            for c in range(CONVS + 1):
                with act.Fori(0, NTURNS) as i:
                    for s in range(B):
                        n = (i + c * NTURNS) * B + s
                        if c in (0, 2):
                            k = (i + (c // 2) * NTURNS) * B + s
                            act.wait_ge(var_made, k + 1)
                            nc.scalar.activation(std[:, :], mv[:, 1:2], ACT.Sqrt, bias=epsc[:, 0:1]).then_inc(std_made, 1)
                        if c < CONVS:
                            act.wait_ge(feat_turned, n + 1)
                            act.wait_ge(prod_made, n + 1)
                            nc.scalar.copy(featT[:, s % 2, :], ps_msg[s % 2][0:D, 0:P]).then_inc(featT_copied, 1)
                            act.wait_ge(prod_made, n + 3)
                            if s in (0, H):
                                act.wait_ge(table_stored[s // H], (i + c * NTURNS) * 16 + 16)
                            nc.scalar.copy(msg[:, s, :], ps_msg[2 + s % 2][:, 0:D]).then_inc(msg_copied, 1)
                if c == CONVS:
                    break
                with act.Fori(0, TURNS) as i:
                    def stage(g):
                        act.wait_ge(msgs_made, i * GPI + c * GROUPS + g + 1)
                        nc.scalar.copy(idx[:, g, :], src_i[:, ds((i * GPI + g) * CPG, CPG)]).then_inc(idx_staged, 1)

                    for g in range(GPI):
                        stage(g)
                    for g in range(GPI):
                        n = i * GPI + c * GROUPS + g
                        act.wait_ge(back_made, n + GPI + 1)
                        act.wait_ge(back_stored[g], (i + c * TURNS) * 16 + 16)
                        nc.scalar.copy(back[:, g, :], ps_back[g % 2][:, 0:CPG * D]).then_inc(back_copied, 1)
                        act.wait_ge(back_copied, n + 3)
                        act.dma_start(
                            scanned_rows[ds((i * GPI + g) * GROUP, GROUP), :].rearrange("(p k) d -> p (k d)", k=CPG),
                            back[:, g, :]).then_inc(back_stored[g], 16)

        @block.tensor
        def _(pe):
            pe.sem_inc(msgs_made, GPI)
            pe.sem_inc(back_made, GPI)
            pe.sem_inc(prod_made, 2)
            pe.sem_inc(hot_used, 1)
            pe.wait_ge(weights_in, 16 * W_DMAS)
            pe.wait_ge(pool_const, 2)
            for c in range(CONVS):
                with pe.Fori(0, NTURNS) as i:
                    for s in range(B):
                        n = (i + c * NTURNS) * B + s
                        pe.wait_ge(feat_made, n + B + 1)
                        pe.wait_ge(featT_copied, n + 1)
                        nc.tensor.transpose(ps_msg[s % 2][0:D, 0:P], feat[:, s, :], ident[:, :]).then_inc(feat_turned, 1)
                        pe.wait_ge(featT_copied, n + 3)
                        pe.wait_ge(msg_copied, n + 1)
                        pe.wait_ge(root_made, n + 1)
                        nc.tensor.matmul(ps_msg[2 + s % 2][:, 0:D], featT[:, s % 2, :], w_cat[c][:, 0:D],
                                         start=True, stop=True)
                        nc.tensor.matmul(ps_back[s % 2][:, 0:D], featT[:, s % 2, :], w_cat[c][:, D:2 * D],
                                         start=True, stop=True).then_inc(prod_made, 1)
                if c == 0:
                    nc.tensor.matmul(ps_deg[:, 0:NT], zbf[:, :], zbf[:, 0:NT], start=True, stop=False)
                with pe.Fori(0, TURNS) as i:
                    def gather_in(g):
                        n = i * GPI + c * GROUPS + g
                        pe.wait_ge(scan_done, n + 1)
                        if c in MAXC:
                            if g == 0:
                                pe.wait_ge(attr_in, (i + c * TURNS + 1) * 16)
                            nc.tensor.matmul(ps_msg[g][0:D, :], w_edge[c][:, g, :], attr[:, :], start=True, stop=False)
                        pe.wait_ge(gathered[g], (i + c * TURNS + 1) * (16 * CPG))
                        for k in range(CPG):
                            o = ps_msg[g][0:D, k * CHUNK:(k + 1) * CHUNK]
                            if c in MAXC:
                                last = nc.tensor.matmul(o, rows[:, g, k, :], ident[:, :], start=False, stop=k == CPG - 1)
                            else:
                                last = nc.tensor.transpose(o, rows[:, g, k, :], ident[:, :])
                        last.then_inc(msgs_made, 1)

                    def scan_out(g):
                        n = i * GPI + c * GROUPS + g
                        pe.wait_ge(scan_done, n + GPI + 1)
                        pe.wait_ge(back_copied, n + 1)
                        for k in range(CPG):
                            last = nc.tensor.transpose(ps_back[g % 2][:, k * D:(k + 1) * D],
                                                       scan[:, g, k * CHUNK:(k + 1) * CHUNK], ident[0:D, 0:D])
                        last.then_inc(back_made, 1)

                    if c == 0:
                        pe.wait_ge(hot_made, i + 1)
                        for k in range(GPI * CPG):
                            last = nc.tensor.matmul(ps_deg[:, 0:NT], hot_lo[:, k, :], hot_hi[:, k, :], start=False,
                                                    stop=False)
                        last.then_inc(hot_used, 1)
                    for g in range(GPI):
                        gather_in(g)
                        if g >= 1:
                            scan_out(g - 1)
                    scan_out(GPI - 1)
                if c == 0:
                    nc.tensor.matmul(ps_deg[:, 0:NT], zbf[:, :], zbf[:, 0:NT], start=False, stop=True).then_inc(deg_made, 1)
                    pe.wait_ge(deg_copied, 1)
                    nc.tensor.matmul(ps_cum[:, 0:NT], tri[:, :], deg[:, :], start=True, stop=True)
                    nc.tensor.matmul(ps_cum[:, NT:2 * NT], ones[:, :], deg[:, :], start=True, stop=True).then_inc(cum_made, 1)

        @block.vector
        def _(dve):
            steps = [0, 0]

            def link(ins):
                ins.then_inc(dve_step, 1)
                steps[0] += 1
                dve.wait_ge(dve_step, steps[0])

            dve.sem_inc(scan_done, GPI)
            dve.sem_inc(feat_made, B)
            dve.sem_inc(featT_copied, 2)
            dve.sem_inc(back_copied, 2)
            dve.sem_inc(msg_copied, 2)
            dve.sem_inc(root_made, 2)
            dve.wait_ge(edges_in, 64)
            link(nc.vector.tensor_tensor(line[:, :].bitcast(fp32), line[:, :], prev[:, :], ALU.not_equal))
            nc.vector.tensor_scalar(mask_max[:, :], line[:, :].bitcast(fp32), -BIG, None, ALU.mult)
            nc.vector.tensor_scalar(mask_sum[:, :], line[:, :].bitcast(fp32), -1.0, 1.0, ALU.mult, ALU.add).then_inc(masks_made, 1)
            link(nc.vector.tensor_scalar(prev[:, :], dst_i[:, :], 7, None, ALU.logical_shift_right))
            nc.vector.tensor_copy(hi_b[:, :], prev[:, :])
            link(nc.vector.tensor_scalar(line[:, :], dst_i[:, :], P - 1, None, ALU.bitwise_and))
            link(nc.vector.tensor_copy(lo_b[:, :], line[:, :]))
            dve.wait_ge(pool_const, 2)
            link(nc.vector.tensor_copy(iota_b[:, :], iota_i[:, :]))
            dve.wait_ge(nodes_in, 32)
            dve.wait_ge(weights_in, 16 * W_DMAS)

            def node_pass(c):
                links = [0]
                per = {0: 5, 1: 2, 2: 8, 3: 3, 4: 3}[c]
                base = steps[0]
                with dve.Fori(0, NTURNS) as i:
                    def hop(ins, s):
                        ins.then_inc(dve_step, 1)
                        links[0] += 1
                        dve.wait_ge(dve_step, i * (per * B) + base + links[0])

                    for s in range(B):
                        n = (i + c * NTURNS) * B + s
                        t = ds(i * B + s, 1)
                        f = feat[:, s, :]
                        if c > 0:
                            h = s // H
                            dve.wait_ge(agg_in[h], (i + (c - 1) * NTURNS) * (16 * H) + 16 * H)
                            r = root[:, t, :].rearrange("p t d -> p (t d)")
                            if c in (1, 2):
                                hop(nc.vector.tensor_tensor(tmp[:, :], agg[:, s, :], r, ALU.add), s)
                            else:
                                hop(nc.vector.tensor_scalar(agg[:, s, :], agg[:, s, :], inv_deg[:, t], None, ALU.mult), s)
                                hop(nc.vector.tensor_tensor(tmp[:, :], agg[:, s, :], r, ALU.add), s)
                        xt = xs[:, t, :].rearrange("p t d -> p (t d)")
                        if c == 1:
                            hop(nc.vector.scalar_tensor_tensor(f, tmp[:, :], 0.01, tmp[:, :], ALU.mult, ALU.max), s)
                        if c == 2:
                            hop(nc.vector.scalar_tensor_tensor(tmp[:, :], tmp[:, :], 0.01, tmp[:, :], ALU.mult, ALU.max), s)
                            hop(nc.vector.tensor_tensor(xt, xt, tmp[:, :], ALU.add), s)
                        if c in (0, 2):
                            k = (i + (c // 2) * NTURNS) * B + s
                            dve.sem_inc(dve_passed, 1)
                            hop(nc.vector.bn_stats(stats[:, :], xt), s)
                            dve.sem_inc(dve_passed, 1)
                            hop(nc.vector.bn_aggr(mv[:, :], stats[:, :]), s)
                            dve.sem_inc(var_made, 1)
                            dve.wait_ge(std_made, k + 1)
                            hop(nc.vector.reciprocal(rstd[:, :], std[:, :]), s)
                            hop(nc.vector.tensor_scalar(tmp[:, :], xt, mv[:, 0:1], rstd[:, 0:1], ALU.subtract, ALU.mult), s)
                            hop(nc.vector.tensor_scalar(f, tmp[:, :], 0.0, None, ALU.max), s)
                        if c == 3:
                            hop(nc.vector.tensor_scalar(f, tmp[:, :], 0.0, None, ALU.max), s)
                        if c == 4:
                            hop(nc.vector.tensor_tensor(y[:, t, :].rearrange("p t d -> p (t d)"), tmp[:, :], xt, ALU.add), s)
                        dve.sem_inc(feat_made, 1)
                        if c < CONVS:
                            dve.wait_ge(prod_made, n + 3)
                            nc.vector.tensor_tensor(root[:, t, :].rearrange("p t d -> p (t d)"),
                                                    ps_back[s % 2][:, 0:D], bias[c][:, :], ALU.add).then_inc(root_made, 1)
                assert links[0] == per * B, (c, links[0])
                steps[0] = base + per * B * NTURNS

            for c in range(CONVS):
                node_pass(c)
                with dve.Fori(0, TURNS) as i:
                    if c == 0:
                        dve.wait_ge(hot_used, i + 1)
                        k0 = i * (GPI * CPG)
                        K = GPI * CPG
                        nc.vector.tensor_tensor(
                            hot_lo[:, :, :],
                            lo_b[:, ds(k0, K)].rearrange("p (k a) -> p k a", a=1).to_broadcast([P, K, P]),
                            iota_b[:, :].rearrange("p (a m) -> p a m", a=1).to_broadcast([P, K, P]), ALU.is_equal)
                        nc.vector.tensor_tensor(
                            hot_hi[:, :, :],
                            hi_b[:, ds(k0, K)].rearrange("p (k a) -> p k a", a=1).to_broadcast([P, K, NT]),
                            iota_b[:, 0:NT].rearrange("p (a m) -> p a m", a=1).to_broadcast([P, K, NT]),
                            ALU.is_equal).then_inc(hot_made, 1)
                    for g in range(GPI):
                        n = i * GPI + c * GROUPS + g
                        dve.wait_ge(mask_in[g], (i + c * TURNS + 1) * 16)
                        dve.wait_ge(msgs_made, n + GPI + 1)
                        dve.wait_ge(back_made, n + 1)
                        dve.wait_ge(scan_done, n + GPI)
                        nc.vector.tensor_tensor_scan(
                            scan[:, g, :], mask[:, g, :], ps_msg[g][0:D, :], scan[:, (g - 1) % GPI, GROUP - 1:GROUP],
                            ALU.add if c in MAXC else ALU.mult,
                            ALU.max if c in MAXC else ALU.add).then_inc(scan_done, 1)
                if c == 0:
                    dve.wait_ge(deg_made, 1)
                    nc.vector.tensor_copy(deg[:, :], ps_deg[:, 0:NT]).then_inc(deg_copied, 1)
                    dve.wait_ge(cum_made, 1)
                    link(nc.vector.tensor_copy(tot[:, :], ps_cum[:, NT:2 * NT]))
                    link(nc.vector.tensor_tensor_scan(pre[:, :], ones[:, 0:NT], tot[:, :], 0.0, ALU.mult, ALU.add))
                    link(nc.vector.tensor_tensor(pre[:, :], pre[:, :], tot[:, :], ALU.subtract))
                    link(nc.vector.tensor_tensor(endf[:, :], ps_cum[:, 0:NT], pre[:, :], ALU.add))
                    link(nc.vector.tensor_scalar(endf[:, :], endf[:, :], -1.0, 0.0, ALU.add, ALU.max))
                    link(nc.vector.tensor_copy(end_i[:, :], endf[:, :]))
                    link(nc.vector.tensor_scalar(part[:, :], end_i[:, :], 9, 9, ALU.logical_shift_right, ALU.logical_shift_left))
                    link(nc.vector.tensor_scalar(part2[:, :], end_i[:, :], P - 1, 2, ALU.bitwise_and, ALU.logical_shift_left))
                    link(nc.vector.tensor_tensor(part[:, :], part[:, :], part2[:, :], ALU.bitwise_or))
                    link(nc.vector.tensor_scalar(part2[:, :], end_i[:, :], 7, CPG - 1, ALU.logical_shift_right, ALU.bitwise_and))
                    link(nc.vector.tensor_tensor(part[:, :], part[:, :], part2[:, :], ALU.bitwise_or))
                    link(nc.vector.tensor_scalar(nonzero[:, :], deg[:, :], 0.0, None, ALU.is_gt))
                    link(nc.vector.tensor_scalar(endf[:, :], part[:, :], -float(ZROW), None, ALU.add))
                    link(nc.vector.tensor_tensor(endf[:, :], endf[:, :], nonzero[:, :], ALU.mult))
                    link(nc.vector.tensor_scalar(end_row[:, :], endf[:, :], float(ZROW), None, ALU.add))
                    link(nc.vector.tensor_scalar(inv_deg[:, :], deg[:, :], 1.0, None, ALU.max))
                    link(nc.vector.reciprocal(inv_deg[:, :], inv_deg[:, :]))
                    dve.sem_inc(end_rows_made, 1)
            node_pass(CONVS)
            dve.sem_inc(out_made, 1)


_INS = ["x", "src_t", "dst_t", "dst_line", "attr_t",
        "L0_gnn_W1_msg", "L0_gnn_W1_edge", "L0_gnn_W1_root", "L0_gnn_b1",
        "L0_gnn_W2_msg", "L0_gnn_W2_edge", "L0_gnn_W2_root", "L0_gnn_b2",
        "L1_gnn_W_self1", "L1_gnn_W_neigh1", "L1_gnn_b1",
        "L1_gnn_W_self2", "L1_gnn_W_neigh2", "L1_gnn_b2"]


def kernel(**inputs):
    import numpy as np
    import concourse.bacc as _bacc
    from concourse import mybir as _mybir
    from concourse.bass_utils import run_bass_kernel_spmd as _run

    a = {k: np.asarray(v) for k, v in inputs.items()}
    src = np.concatenate([a["src"], np.zeros(EP - E, a["src"].dtype)])
    dst = np.concatenate([a["dst"], np.full(EP - E, N, a["dst"].dtype)])
    a["src_t"] = src.reshape(CHUNKS, P).T
    a["dst_t"] = dst.reshape(CHUNKS, P).T
    a["dst_line"] = np.concatenate([np.full(1, -1, dst.dtype), dst])
    attr = np.concatenate([a["edge_attr_32"], np.zeros((EP - E, DA), a["edge_attr_32"].dtype)])
    a["attr_t"] = attr.reshape(TURNS, GPI, GROUP, DA).transpose(0, 1, 3, 2).reshape(TURNS * P, GROUP)

    nc = _bacc.Bacc("TRN2", target_bir_lowering=False, num_devices=1)
    arrays, args = {}, []
    for name in _INS:
        v = np.ascontiguousarray(a[name])
        arrays[f"in_{name}_dram"] = v
        args.append(nc.dram_tensor(f"in_{name}_dram", v.shape, _mybir.dt.from_np(v.dtype), kind="ExternalInput").ap())
    args.append(nc.dram_tensor("out_0_dram", (N, D), _mybir.dt.float32, kind="ExternalOutput").ap())
    gnn_kernel(nc, *args)
    r = _run(nc, [arrays], core_ids=[0])
    return r.results[0]["out_0_dram"]
```

```python
import concourse.bass as bass
from concourse import mybir
from contextlib import ExitStack


N = 6250
D = 96
DA = 32
E = 206250
P = 128
CHUNK = P
CPG = 4
GROUP = CPG * CHUNK
GPI = 4
TURN = GPI * GROUP
TURNS = -(-E // TURN)
EP = TURNS * TURN
CHUNKS = EP // CHUNK
GROUPS = EP // GROUP
B = 10
H = B // 2
NT = -(-N // (B * P)) * B
NTURNS = NT // B
HALVES = NT // H
FULL = N // P
REST = N - FULL * P
HI = FULL + 1
PADN = NT * P - 1
ZROW = EP
BIG = 3.3895313892515355e38
EPS = 1e-5
CONVS = 4
MAXC = (0, 1)
WIN = 8
WCH = 4
WIN_CAP = WCH * CHUNK
KEYS = HI * WIN
WPT = 2 * GPI
HS = WPT * WIN
WB = 7
NWIN = -(-N // WIN)
RPT = WB * WIN + 1
DEG_CAP = 256
SLABS = 5
PARTS = 3
EROWS = CHUNKS + WCH

def gnn_kernel(nc: bass.Bass, x, src_t, dst_t, dst_line, edges_packed, attr_t,
               w_msg1, w_edge1, w_root1, b1, w_msg2, w_edge2, w_root2, b2,
               s_self1, s_neigh1, sb1, s_self2, s_neigh2, sb2, out):
    fp32 = mybir.dt.float32
    bf16 = mybir.dt.bfloat16
    fp16 = mybir.dt.float16
    i32 = mybir.dt.int32
    ALU = mybir.AluOpType
    ACT = mybir.ActivationFunctionType
    AX = mybir.AxisListType
    ds = bass.ds

    table = nc.dram_tensor("table", (NT * P, D), fp32, kind="Internal").ap()
    scanned_rows = nc.dram_tensor("scanned_rows", (EP + 7, D), fp32, kind="Internal").ap()
    masks = nc.dram_tensor("masks", (2, EP), bf16, kind="Internal").ap()
    firsts = nc.dram_tensor("firsts", (RPT, P), fp32, kind="Internal").ap()
    slabs = nc.dram_tensor("slabs", (NT, P, HI * P), bf16, kind="Internal").ap()

    ctx = ExitStack()
    with ctx:
        def sb(name, shape, dt=fp32, scope=ctx):
            return scope.enter_context(nc.sbuf_tensor(name, shape, dt))

        def sem(name):
            return ctx.enter_context(nc.semaphore(name))

        ident = sb("ident", [P, P])
        tri = sb("tri", [P, P])
        ones = sb("ones", [P, P])
        zbf = sb("zbf", [P, P], bf16)
        zrow = sb("zrow", [1, D])
        win_node = sb("win_node", [P, WB], i32)
        w_cat = [sb(f"w_cat{c}", [D, 2 * D]) for c in range(CONVS)]
        w_edge = [sb(f"w_edge{c}", [P, GPI, D]) for c in MAXC]
        bias = [sb(f"bias{c}", [P, D]) for c in range(CONVS)]
        iota_k = sb("iota_k", [P, KEYS], fp16)
        src_i = sb("src_i", [P, CHUNKS + GPI * CPG], i32)
        xs = sb("xs", [P, NT, D])
        root = sb("root", [P, NT, D])
        deg = sb("deg", [P, NT])
        inv_deg = sb("inv_deg", [P, NT])
        end_row = sb("end_row", [P, NT], i32)
        end_idx = sb("end_idx", [P, B], i32)
        agg = sb("agg", [P, B, D])
        feat = sb("feat", [P, B, D])
        tmp = sb("tmp", [P, H, D])
        cent = sb("cent", [P, H, D])
        mean5 = sb("mean5", [P, H])
        var5 = sb("var5", [P, H])
        std5 = sb("std5", [P, H])
        rstd5 = sb("rstd5", [P, H])
        featT = sb("featT", [D, 2, H * P])
        ok_i = sb("ok_i", [1, 1], i32)
        early = ExitStack()
        with early:
            dst_i = sb("dst_i", [P, CHUNKS], i32, early)
            line = sb("line", [P, CHUNKS], i32, early)
            prev = sb("prev", [P, CHUNKS], i32, early)
            hi_b = sb("hi_b", [P, CHUNKS], bf16, early)
            lo_b = sb("lo_b", [P, CHUNKS], bf16, early)
            mask_max = sb("mask_max", [P, CHUNKS], bf16, early)
            mask_sum = sb("mask_sum", [P, CHUNKS], bf16, early)
            iota_i = sb("iota_i", [P, KEYS], i32, early)
            iota_b = sb("iota_b", [P, P], bf16, early)
        prep = ExitStack()
        with prep:
            first_all = sb("first_all", [P, RPT], scope=prep)
            cnt = {n: sb(n, [P, NT], scope=prep) for n in ("tot", "pre", "endf", "nonzero")}
            end_i = sb("end_i", [P, NT], i32, prep)
            part = sb("part", [P, NT], i32, prep)
            part2 = sb("part2", [P, NT], i32, prep)
            first_t = sb("first_t", [RPT, P], scope=prep)
            win_at = sb("win_at", [P, 2, WB, WIN], scope=prep)
            row_i = sb("row_i", [P, WB], i32, prep)
            row_f = sb("row_f", [P, WB], scope=prep)
            lim_f = sb("lim_f", [P, WB], scope=prep)
            row_idx = sb("row_idx", [P, WB, WCH], i32, prep)
            bad = sb("bad", [P, 2], scope=prep)
            bad_w = sb("bad_w", [P, WB], scope=prep)
            bad_d = sb("bad_d", [P, HI], scope=prep)
            krow = sb("krow", [P, WCH, 2 * CHUNK], i32, prep)
            k_loc = sb("k_loc", [P, WCH, CHUNK], i32, prep)
            k_a = sb("k_a", [P, WCH, CHUNK], i32, prep)
            k_v = sb("k_v", [P, WCH, CHUNK], scope=prep)
            k_key = sb("k_key", [P, WCH, CHUNK], scope=prep)
            k_lo = sb("k_lo", [P, WCH, CHUNK], scope=prep)
        hparts = [sb(f"hparts{j}", [P, NT, PARTS * D], bf16) for j in range(2)]
        sparse = ExitStack()
        with sparse:
            idx = sb("idx", [P, GPI, CPG], i32, sparse)
            rows = sb("rows", [P, GPI, CPG, D], scope=sparse)
            attr = sb("attr", [P, GROUP], scope=sparse)
            mask = sb("mask", [D, GPI, GROUP], bf16, sparse)
            scan = sb("scan", [D, GPI, GROUP], scope=sparse)
            back = sb("back", [P, GPI, CPG * D], scope=sparse)
            msg = sb("msg", [P, B, D], scope=sparse)
            hist = ExitStack()
            with hist:
                hot_lo = sb("hot_lo", [P, GPI * CPG, P], bf16, hist)
                hot_hi = sb("hot_hi", [P, GPI * CPG, NT], bf16, hist)
            win_lo = sb("win_lo", [P, 2, WCH, P], bf16, sparse)
            win_key = sb("win_key", [P, 2, WCH, KEYS], bf16, sparse)
            new_slab = sb("new_slab", [P, HI, P], bf16, sparse)
            keyT = sb("keyT", [P, WB * P * WCH], scope=sparse)
            loT = sb("loT", [P, WB * P * WCH], scope=sparse)
        slab = sb("slab", [P, SLABS, HI, P], bf16)
        resid = sb("resid", [P, 2, H * D])

        psum = ctx.enter_context(nc.psum_tensor("psum", [P, 8, GROUP], fp32))
        ps_msg = [psum[:, j, :] for j in (0, 1)]
        ps_back = [psum[:, j, :] for j in (2, 3)]
        ps_win = [psum[:, j, :] for j in (4, 5)]
        ps_deg = psum[:, 6, :]
        ps_cum = psum[:, 7, :]
        ps_turned = psum[:, 0:2, :].rearrange("p a b -> p (a b)")
        ps_m = [psum[:, j, :] for j in (2, 3)]
        ps_r = [psum[:, j, :] for j in (6, 7)]

        weights_in = sem("weights_in")
        edges_in = sem("edges_in")
        nodes_in = sem("nodes_in")
        zeroed = sem("zeroed")
        masks_made = sem("masks_made")
        masks_stored = sem("masks_stored")
        pool_const = sem("pool_const")
        dve_step = sem("dve_step")
        pool_passed = sem("pool_passed")
        dve_passed = sem("dve_passed")
        act_passed = sem("act_passed")
        hot_made = sem("hot_made")
        hot_used = sem("hot_used")
        deg_made = sem("deg_made")
        deg_copied = sem("deg_copied")
        cum_made = sem("cum_made")
        end_rows_made = sem("end_rows_made")
        firsts_made = sem("firsts_made")
        firsts_turned = sem("firsts_turned")
        firsts_copied = sem("firsts_copied")
        firsts_stored = sem("firsts_stored")
        firsts_in = sem("firsts_in")
        rows_known = sem("rows_known")
        krow_in = sem("krow_in")
        krow_used = sem("krow_used")
        keys_made = sem("keys_made")
        keys_turned = sem("keys_turned")
        keys_copied = sem("keys_copied")
        bad_made = sem("bad_made")
        bad_summed = sem("bad_summed")
        ok_known = sem("ok_known")
        wins_hot = sem("wins_hot")
        wins_made = sem("wins_made")
        wins_copied = sem("wins_copied")
        slab_stored = sem("slab_stored")
        idx_staged = sem("idx_staged")
        gathered = [sem(f"gathered{g}") for g in range(GPI)]
        attr_in = sem("attr_in")
        mask_in = [sem(f"mask_in{g}") for g in range(GPI)]
        msgs_made = sem("msgs_made")
        scan_done = sem("scan_done")
        back_made = sem("back_made")
        back_copied = sem("back_copied")
        back_stored = [sem(f"back_stored{g}") for g in range(GPI)]
        end_staged = sem("end_staged")
        agg_in = [sem(f"agg_in{h}") for h in range(2)]
        feats_made = sem("feats_made")
        feats_turned = sem("feats_turned")
        featT_copied = sem("featT_copied")
        prods_made = sem("prods_made")
        prods_taken = sem("prods_taken")
        roots_made = sem("roots_made")
        table_stored = [sem(f"table_stored{h}") for h in range(2)]
        var_made = sem("var_made")
        std_made = sem("std_made")
        part1_made = sem("part1_made")
        resid_made = sem("resid_made")
        part2_made = sem("part2_made")
        parts_made = sem("parts_made")
        slab_in = [sem(f"slab_in{j}") for j in range(SLABS)]
        dense_made = sem("dense_made")
        dense_used = sem("dense_used")
        out_made = sem("out_made")
        out_stored = sem("out_stored")

        block = ctx.enter_context(nc.Block())

        W_DMAS = 2 * CONVS + GPI * len(MAXC) + CONVS

        def half_no(i, p, h):
            return i * 2 + (p * HALVES + h)

        def group_no(i, c, g):
            return i * GPI + (c * GROUPS + g)

        @block.sync
        def _(sp):
            def store_table(c):
                with sp.Fori(0, NTURNS) as i:
                    for h in range(2):
                        sp.wait_ge(prods_taken, half_no(i, c, h) + 3)
                        sp.dma_start(
                            table[ds(i * (B * P) + h * H * P, H * P), :].rearrange("(t p) d -> p t d", p=P),
                            msg[:, h * H:(h + 1) * H, :]).then_inc(table_stored[h], 16)

            def edge_loads(c):
                with sp.Fori(0, TURNS) as i:
                    for g in range(GPI):
                        if g == 0 and c in MAXC:
                            sp.wait_ge(msgs_made, group_no(i, c, GPI))
                            sp.dma_start(attr[:, :], attr_t[ds(i * P, P), :]).then_inc(attr_in, 16)
                        sp.wait_ge(scan_done, group_no(i, c, g + 1))
                        m = masks[0 if c in MAXC else 1, ds(i * TURN + g * GROUP, GROUP)]
                        sp.dma_start(mask[:, g, :], m.rearrange("(a e) -> a e", a=1).to_broadcast([D, GROUP])).then_inc(mask_in[g], 16)

            def slab_loads(c):
                with sp.Fori(0, NTURNS) as i:
                    for s in range(B):
                        t = i * B + ((c - 2) * NT + s)
                        sp.wait_ge(dense_made, t + 1)
                        sp.dma_start(slab[:, s % SLABS].rearrange("p k d -> p (k d)"),
                                     slabs[ds(i * B + s, 1), :, :].rearrange("a p n -> p (a n)")).then_inc(slab_in[s % SLABS], 16)

            sp.wait_ge(zeroed, 1)
            sp.dma_start(line[:, :], dst_line[1:1 + EP].rearrange("(p c) -> p c", p=P)).then_inc(edges_in, 16)
            sp.dma_start(prev[:, :], dst_line[0:EP].rearrange("(p c) -> p c", p=P)).then_inc(edges_in, 16)
            sp.dma_start(xs[:, 0:FULL, :], x[0:FULL * P, :].rearrange("(t p) d -> p t d", p=P)).then_inc(nodes_in, 16)
            sp.dma_start(xs[0:REST, FULL, :], x[FULL * P:N, :]).then_inc(nodes_in, 16)
            for c, (wm, wr, b) in enumerate([(w_msg1, w_root1, b1), (w_msg2, w_root2, b2),
                                             (s_neigh1, s_self1, sb1), (s_neigh2, s_self2, sb2)]):
                sp.dma_start(w_cat[c][:, 0:D], wm).then_inc(weights_in, 16)
                sp.dma_start(w_cat[c][:, D:2 * D], wr).then_inc(weights_in, 16)
                sp.dma_start(bias[c][:, :], b.rearrange("(a d) -> a d", a=1).to_broadcast([P, D])).then_inc(weights_in, 16)
            for c, we in enumerate([w_edge1, w_edge2]):
                for g in range(GPI):
                    sp.dma_start(w_edge[c][DA * g:DA * g + DA, g, :], we).then_inc(weights_in, 16)
            for j, stored in enumerate(back_stored + table_stored + [slab_stored]):
                sp.dma_start(scanned_rows[ZROW + j:ZROW + j + 1, :], zrow[0:1, :]).then_inc(stored, 16)
            sp.dma_start(src_i[:, 0:CHUNKS], src_t).then_inc(edges_in, 16)
            sp.dma_start(dst_i[:, :], dst_t).then_inc(edges_in, 16)
            sp.wait_ge(masks_made, 1)
            sp.dma_start(masks[0, :].rearrange("(p c) -> p c", p=P), mask_max[:, :]).then_inc(masks_stored, 16)
            sp.dma_start(masks[1, :].rearrange("(p c) -> p c", p=P), mask_sum[:, :]).then_inc(masks_stored, 16)
            sp.wait_ge(masks_stored, 32)
            store_table(0)
            edge_loads(0)
            sp.wait_ge(firsts_copied, 1)
            sp.dma_start(firsts, first_t[:, :]).then_inc(firsts_stored, 16)
            sp.wait_ge(firsts_stored, 16)
            flat = firsts.rearrange("t p -> (t p)")
            for j in range(2):
                sp.dma_start(win_at[:, j], flat[j * WIN:j * WIN + WB * P * WIN].rearrange("(b p w) -> p b w", p=P, w=WIN)).then_inc(firsts_in, 16)
            store_table(1)
            edge_loads(1)
            sp.wait_ge(ok_known, 1)
            ok = sp.value_load(ok_i[0:1, 0:1])
            with sp.If(ok):
                sp.wait_ge(slab_stored, 16 * (NT + 1))
                sp.wait_ge(feats_made, 2 * HALVES + 1)
                slab_loads(2)
                slab_loads(3)
            with sp.Else():
                for c in (2, 3):
                    store_table(c)
                    edge_loads(c)
            sp.wait_ge(out_made, 1)
            sp.dma_start(out[0:FULL * P, :].rearrange("(t p) d -> p t d", p=P), xs[:, 0:FULL, :]).then_inc(out_stored, 16)
            sp.dma_start(out[FULL * P:N, :], xs[0:REST, FULL, :]).then_inc(out_stored, 16)
            sp.wait_ge(out_stored, 32)

        @block.gpsimd
        def _(pool):
            def gather_edges(c):
                pool.wait_ge(table_stored[0], 16 * NTURNS * (c + 1) + 16)
                pool.wait_ge(table_stored[1], 16 * NTURNS * (c + 1) + 16)
                with pool.Fori(0, TURNS) as i:
                    for g in range(GPI):
                        n = group_no(i, c, g)
                        pool.wait_ge(idx_staged, n + (c * GPI + 1))
                        pool.wait_ge(msgs_made, n + 1)
                        pool.sem_inc(pool_passed, 1)
                        for k in range(CPG):
                            pool.indirect_dma_start(
                                rows[:, g, k, :], None, table,
                                bass.IndirectOffsetOnAxis(ap=idx[:, g, k:k + 1], axis=0)).then_inc(gathered[g], 16)

            def gather_ends(c):
                for g in range(GPI):
                    pool.wait_ge(back_stored[g], 16 * TURNS * (c + 1) + 16)
                pool.wait_ge(end_rows_made, 1)
                with pool.Fori(0, NTURNS) as i:
                    for h in range(2):
                        pool.wait_ge(feats_made, half_no(i, c + 1, h) - 1)
                        pool.tensor_copy(end_idx[:, h * H:(h + 1) * H], end_row[:, ds(i * B + h * H, H)]).then_inc(end_staged, 1)
                        pool.wait_ge(end_staged, half_no(i, c, h) + 1)
                        pool.sem_inc(pool_passed, 1)
                        for s in range(h * H, (h + 1) * H):
                            pool.indirect_dma_start(
                                agg[:, s, :], None, scanned_rows,
                                bass.IndirectOffsetOnAxis(ap=end_idx[:, s:s + 1], axis=0)).then_inc(agg_in[h], 16)

            pool.memset(xs[:, FULL:NT, :], 0.0)
            pool.memset(src_i[:, CHUNKS:], 0)
            pool.memset(zrow[:, :], 0.0)
            pool.memset(w_edge[0][:, :, :], 0.0)
            pool.memset(w_edge[1][:, :, :], 0.0)
            pool.memset(scan[:, :, :], 0.0).then_inc(zeroed, 1)
            pool.memset(zbf[:, :], 0.0)
            pool.memset(ones[:, :], 1.0)
            pool.memset(ident[:, :], 0.0).then_inc(pool_const, 1)
            pool.wait_ge(pool_const, 1)
            pool.affine_select(out=ident[:, :], in_=ident[:, :], compare_op=ALU.not_equal, fill=1.0,
                               base=0, pattern=[[-1, P]], channel_multiplier=1)
            pool.affine_select(out=tri[:, :], in_=ones[:, :], compare_op=ALU.is_ge, fill=0.0,
                               base=0, pattern=[[1, P]], channel_multiplier=-1)
            pool.iota(win_node[:, :], pattern=[[P * WIN, WB]], base=0, channel_multiplier=WIN)
            pool.iota(iota_i[:, :], pattern=[[1, KEYS]], base=0, channel_multiplier=0).then_inc(pool_const, 1)
            gather_edges(0)
            gather_ends(0)
            pool.wait_ge(rows_known, 1)
            pool.affine_select(out=bad_w[:, :], in_=bad_w[:, :], compare_op=ALU.is_ge, fill=0.0,
                               base=NWIN - 1, pattern=[[-P, WB]], channel_multiplier=-1).then_inc(rows_known, 1)
            for b in range(WB):
                if b >= 1:
                    pool.wait_ge(krow_used, b)
                for r in range(WCH):
                    pool.indirect_dma_start(
                        krow[:, r, :], None, edges_packed,
                        bass.IndirectOffsetOnAxis(ap=row_idx[:, b, r:r + 1], axis=0)).then_inc(krow_in, 16)
            gather_edges(1)
            gather_ends(1)
            pool.wait_ge(ok_known, 1)
            ok = pool.value_load(ok_i[0:1, 0:1])
            with pool.If(ok):
                pool.sem_inc(pool_passed, 1)
            with pool.Else():
                for c in (2, 3):
                    gather_edges(c)
                    gather_ends(c)

        @block.scalar
        def _(act):
            def node_pass(p, dense):
                with act.Fori(0, NTURNS) as i:
                    for h in range(2):
                        n = half_no(i, p, h)
                        hb = slice(h * H, (h + 1) * H)
                        if p in (0, 2):
                            act.wait_ge(var_made, half_no(i, p // 2, h) + 1)
                            nc.scalar.activation(std5[:, :], var5[:, :], ACT.Sqrt).then_inc(std_made, 1)
                        act.wait_ge(feats_turned, n + 3)
                        act.wait_ge(prods_made, n + 1)
                        nc.scalar.copy(featT[:, h, 0:GROUP], ps_turned[0:D, 0:GROUP])
                        nc.scalar.copy(featT[:, h, GROUP:H * P], ps_turned[0:D, GROUP:H * P]).then_inc(featT_copied, 1)
                        act.wait_ge(prods_made, n + 3)
                        m = ps_m[h][:, 0:H * D].rearrange("p (t d) -> p t d", d=D)
                        if dense:
                            q = p - 2
                            r = resid[:, h, :].rearrange("p (t d) -> p t d", d=D)
                            act.sem_inc(act_passed, 1)
                            nc.scalar.copy(hparts[q][:, ds(i * B + h * H, H), 0:D], m).then_inc(part1_made, 1)
                            act.wait_ge(resid_made, half_no(i, q, h) + 1)
                            act.sem_inc(act_passed, 1)
                            nc.scalar.copy(hparts[q][:, ds(i * B + h * H, H), D:2 * D], r).then_inc(part2_made, 1)
                        else:
                            act.wait_ge(table_stored[h], (i + p * NTURNS) * 16 + 16)
                            nc.scalar.copy(msg[:, hb, :], m).then_inc(prods_taken, 1)

            def edge_turn(i, c, half):
                for g in range(GPI):
                    n = group_no(i, c, g)
                    act.wait_ge(msgs_made, n + GPI + 1)
                    nc.scalar.copy(idx[:, g, :], src_i[:, ds(i * (GPI * CPG) + (GPI + g) * CPG, CPG)]).then_inc(idx_staged, 1)
                    if half is not None:
                        for w in (2 * g, 2 * g + 1):
                            act.wait_ge(wins_made, i * WPT + w + 3)
                            if (half, w) == (0, 0):
                                act.wait_ge(slab_stored, i * 8 + 16)
                            nc.scalar.copy(new_slab[:, :, ds(half * HS + w * WIN, WIN)],
                                           ps_win[w % 2][:, 0:KEYS].rearrange("p (k d) -> p k d", d=WIN)).then_inc(wins_copied, 1)
                    act.wait_ge(back_made, n + GPI + 1)
                    act.wait_ge(back_stored[g], (i + c * TURNS) * 16 + 16)
                    nc.scalar.copy(back[:, g, :], ps_back[g % 2][:, 0:CPG * D]).then_inc(back_copied, 1)
                    act.wait_ge(back_copied, n + 3)
                    act.dma_start(
                        scanned_rows[ds(i * TURN + g * GROUP, GROUP), :].rearrange("(p k) d -> p (k d)", k=CPG),
                        back[:, g, :]).then_inc(back_stored[g], 16)

            def first_indices(c):
                act.wait_ge(msgs_made, c * GROUPS + GPI)
                for g in range(GPI):
                    nc.scalar.copy(idx[:, g, :], src_i[:, g * CPG:(g + 1) * CPG]).then_inc(idx_staged, 1)

            def edge_loop(c):
                with act.Fori(0, TURNS) as i:
                    edge_turn(i, c, None)

            def edge_loop_slabs(c):
                with act.Fori(0, NT) as j:
                    for half in range(2):
                        edge_turn(j * 2 + half, c, half)
                    act.wait_ge(wins_copied, j * (2 * WPT) + (2 * WPT + 2))
                    act.dma_start(slabs[ds(j, 1), :, :].rearrange("a p n -> p (a n)"),
                                  new_slab[:, :, :].rearrange("p k d -> p (k d)")).then_inc(slab_stored, 16)
                edge_turn(2 * NT, c, None)

            act.wait_ge(edges_in, 64)
            first_indices(0)
            node_pass(0, False)
            edge_loop(0)
            first_indices(1)
            node_pass(1, False)
            for b in range(WB):
                act.wait_ge(keys_turned, b + 1)
                for o, bank in ((keyT, 0), (loT, 1)):
                    last = nc.scalar.copy(
                        o[:, b * WIN_CAP:(b + 1) * WIN_CAP].rearrange("p (w r) -> p r w", r=WCH),
                        ps_msg[bank].rearrange("p (r w) -> p r w", r=WCH))
                last.then_inc(keys_copied, 1)
            edge_loop_slabs(1)
            act.wait_ge(ok_known, 1)
            ok = act.value_load(ok_i[0:1, 0:1])
            with act.If(ok):
                node_pass(2, True)
                node_pass(3, True)
            with act.Else():
                for c in (2, 3):
                    first_indices(c)
                    node_pass(c, False)
                    edge_loop(c)

        @block.tensor
        def _(pe):
            def turn_half(i, p, h):
                n = half_no(i, p, h)
                pe.wait_ge(feats_made, n + 1)
                pe.wait_ge(featT_copied, n + 1)
                for s in range(H):
                    last = nc.tensor.transpose(ps_turned[0:D, s * P:(s + 1) * P], feat[:, h * H + s, :], ident[:, :])
                last.then_inc(feats_turned, 1)

            def multiply_half(i, p, h):
                n = half_no(i, p, h)
                pe.wait_ge(featT_copied, n + 2)
                pe.wait_ge(prods_taken, n + 1)
                pe.wait_ge(roots_made, n + 1)
                for s in range(H):
                    nc.tensor.matmul(ps_m[h][:, s * D:(s + 1) * D], featT[:, h, s * P:(s + 1) * P], w_cat[p][:, 0:D],
                                     start=True, stop=True)
                    last = nc.tensor.matmul(ps_r[h][:, s * D:(s + 1) * D], featT[:, h, s * P:(s + 1) * P],
                                            w_cat[p][:, D:2 * D], start=True, stop=True)
                last.then_inc(prods_made, 1)

            def dense_tile(i, q, s):
                t = i * B + (q * NT + s)
                pe.wait_ge(slab_in[s % SLABS], (i * (B // SLABS) + (q * (NT // SLABS) + s // SLABS + 1)) * 16)
                pe.wait_ge(dense_used, t + 1)
                for k in range(HI):
                    last = nc.tensor.matmul(ps_win[s % 2][:, 0:PARTS * D], slab[:, s % SLABS, k, :],
                                            hparts[q][:, k, :], start=k == 0, stop=k == HI - 1)
                last.then_inc(dense_made, 1)

            def node_pass(p, dense):
                with pe.Fori(0, NTURNS) as i:
                    if dense:
                        for s in range(B):
                            dense_tile(i, p - 3, s)
                    if p < CONVS:
                        for h in range(2):
                            turn_half(i, p, h)
                            multiply_half(i, p, h)

            def edge_turn(i, c, half):
                def gather_in(g):
                    n = group_no(i, c, g)
                    bank = ps_msg[g % 2][0:D, :]
                    pe.wait_ge(scan_done, n + 3)
                    if c in MAXC:
                        if g == 0:
                            pe.wait_ge(attr_in, (i + c * TURNS + 1) * 16)
                        nc.tensor.matmul(bank, w_edge[c][:, g, :], attr[:, :], start=True, stop=False)
                    pe.wait_ge(gathered[g], (i + c * TURNS + 1) * (16 * CPG))
                    for k in range(CPG):
                        o = bank[:, k * CHUNK:(k + 1) * CHUNK]
                        if c in MAXC:
                            last = nc.tensor.matmul(o, rows[:, g, k, :], ident[:, :], start=False, stop=k == CPG - 1)
                        else:
                            last = nc.tensor.transpose(o, rows[:, g, k, :], ident[:, :])
                    last.then_inc(msgs_made, 1)

                def scan_out(g):
                    n = group_no(i, c, g)
                    pe.wait_ge(scan_done, n + GPI + 1)
                    pe.wait_ge(back_copied, n + 1)
                    for k in range(CPG):
                        last = nc.tensor.transpose(ps_back[g % 2][:, k * D:(k + 1) * D],
                                                   scan[:, g, k * CHUNK:(k + 1) * CHUNK], ident[0:D, 0:D])
                    last.then_inc(back_made, 1)

                def window(w):
                    pe.wait_ge(wins_hot, i * WPT + w + 1)
                    pe.wait_ge(wins_copied, i * WPT + w + 1)
                    for r in range(WCH):
                        last = nc.tensor.matmul(ps_win[w % 2][:, 0:KEYS], win_lo[:, w % 2, r, :], win_key[:, w % 2, r, :],
                                                start=r == 0, stop=r == WCH - 1)
                    last.then_inc(wins_made, 1)

                if c == 0:
                    pe.wait_ge(hot_made, i + 1)
                    for k in range(GPI * CPG):
                        last = nc.tensor.matmul(ps_deg[:, 0:NT], hot_lo[:, k, :], hot_hi[:, k, :], start=False,
                                                stop=False)
                    last.then_inc(hot_used, 1)
                for g in range(GPI):
                    gather_in(g)
                    if half is not None:
                        window(2 * g)
                        window(2 * g + 1)
                    if g >= 1:
                        scan_out(g - 1)
                scan_out(GPI - 1)

            def edge_loop(c):
                with pe.Fori(0, TURNS) as i:
                    edge_turn(i, c, None)

            def edge_loop_slabs(c):
                with pe.Fori(0, NT) as j:
                    for half in range(2):
                        edge_turn(j * 2 + half, c, half)
                edge_turn(2 * NT, c, None)

            pe.sem_inc(msgs_made, GPI)
            pe.sem_inc(back_made, GPI)
            pe.sem_inc(feats_turned, 2)
            pe.sem_inc(prods_made, 2)
            pe.sem_inc(hot_used, 1)
            pe.sem_inc(wins_made, 2)
            pe.sem_inc(dense_made, SLABS)
            pe.wait_ge(weights_in, 16 * W_DMAS)
            pe.wait_ge(pool_const, 2)
            node_pass(0, False)
            nc.tensor.matmul(ps_deg[:, 0:NT], zbf[:, :], zbf[:, 0:NT], start=True, stop=False)
            edge_loop(0)
            nc.tensor.matmul(ps_deg[:, 0:NT], zbf[:, :], zbf[:, 0:NT], start=False, stop=True).then_inc(deg_made, 1)
            pe.wait_ge(deg_copied, 1)
            nc.tensor.matmul(ps_cum[:, 0:NT], tri[:, :], deg[:, :], start=True, stop=True)
            nc.tensor.matmul(ps_cum[:, NT:2 * NT], ones[:, :], deg[:, :], start=True, stop=True).then_inc(cum_made, 1)
            pe.wait_ge(firsts_made, 1)
            nc.tensor.transpose(ps_deg[0:RPT, 0:P], first_all[:, :], ident[:, :]).then_inc(firsts_turned, 1)
            node_pass(1, False)
            pe.wait_ge(bad_made, 1)
            nc.tensor.matmul(ps_cum[0:1, 0:1], ones[:, 0:1], bad[:, 0:1], start=True, stop=True).then_inc(bad_summed, 1)
            for b in range(WB):
                pe.wait_ge(keys_made, b + 1)
                if b >= 1:
                    pe.wait_ge(keys_copied, b)
                for bank, k in ((0, k_key), (1, k_lo)):
                    for r in range(WCH):
                        last = nc.tensor.transpose(ps_msg[bank][:, r * P:(r + 1) * P], k[:, r, :], ident[:, :])
                last.then_inc(keys_turned, 1)
            pe.wait_ge(keys_copied, WB)
            edge_loop_slabs(1)
            pe.wait_ge(ok_known, 1)
            ok = pe.value_load(ok_i[0:1, 0:1])
            with pe.If(ok):
                node_pass(2, False)
                pe.wait_ge(parts_made, HALVES)
                node_pass(3, True)
                pe.wait_ge(parts_made, 2 * HALVES)
                node_pass(4, True)
            with pe.Else():
                for c in (2, 3):
                    node_pass(c, False)
                    edge_loop(c)

        @block.vector
        def _(dve):
            steps = [0]

            def link(ins):
                ins.then_inc(dve_step, 1)
                steps[0] += 1
                dve.wait_ge(dve_step, steps[0])

            def bcast(v):
                return v[:, :].rearrange("p (t a) -> p t a", a=1).to_broadcast([P, H, D])

            def node_pass(p, dense_in, dense_out):
                per = {0: 7, 1: 2, 2: 10, 3: 3, 4: 3}[p]
                base = steps[0]
                with dve.Fori(0, NTURNS) as i:
                    seen = [0]

                    def hop(ins):
                        ins.then_inc(dve_step, 1)
                        seen[0] += 1
                        dve.wait_ge(dve_step, i * (2 * per) + (base + seen[0]))

                    if dense_in:
                        for s in range(B):
                            t = i * B + ((p - 3) * NT + s)
                            dve.wait_ge(dense_made, t + (SLABS + 1))
                            nc.vector.tensor_reduce(
                                agg[:, s, :], ps_win[s % 2][:, 0:PARTS * D].rearrange("p (j d) -> p d j", j=PARTS),
                                AX.X, ALU.add).then_inc(dense_used, 1)
                    for h in range(2):
                        n = half_no(i, p, h)
                        hb = slice(h * H, (h + 1) * H)
                        th = ds(i * B + h * H, H)
                        f = feat[:, hb, :]
                        xt = xs[:, th, :]
                        if p > 0:
                            dve.wait_ge(roots_made, n - (HALVES - 3))
                            if dense_in:
                                dve.wait_ge(dense_used, i * B + ((p - 3) * NT + h * H + H + 2))
                            else:
                                dve.wait_ge(agg_in[h], (i + (p - 1) * NTURNS + 1) * (16 * H))
                        if p in (1, 2):
                            hop(nc.vector.tensor_tensor(tmp[:, :, :], agg[:, hb, :], root[:, th, :], ALU.add))
                        if p in (3, 4):
                            hop(nc.vector.tensor_tensor(
                                cent[:, :, :], agg[:, hb, :],
                                inv_deg[:, th].rearrange("p (t a) -> p t a", a=1).to_broadcast([P, H, D]), ALU.mult))
                            hop(nc.vector.tensor_tensor(tmp[:, :, :], cent[:, :, :], root[:, th, :], ALU.add))
                        if p < CONVS:
                            dve.wait_ge(feats_turned, n + 1)
                        if p == 1:
                            hop(nc.vector.scalar_tensor_tensor(f, tmp[:, :, :], 0.01, tmp[:, :, :], ALU.mult, ALU.max))
                        if p == 2:
                            hop(nc.vector.scalar_tensor_tensor(tmp[:, :, :], tmp[:, :, :], 0.01, tmp[:, :, :], ALU.mult, ALU.max))
                            hop(nc.vector.tensor_tensor(xt, xt, tmp[:, :, :], ALU.add))
                        if p in (0, 2):
                            dve.sem_inc(dve_passed, 1)
                            hop(nc.vector.reduce_sum(mean5[:, :], xt, AX.X))
                            hop(nc.vector.tensor_scalar(mean5[:, :], mean5[:, :], 1.0 / D, None, ALU.mult))
                            hop(nc.vector.tensor_tensor(cent[:, :, :], xt, bcast(mean5), ALU.subtract))
                            hop(nc.vector.tensor_tensor(tmp[:, :, :], cent[:, :, :], cent[:, :, :], ALU.mult))
                            hop(nc.vector.reduce_sum(rstd5[:, :], tmp[:, :, :], AX.X))
                            nc.vector.tensor_scalar(var5[:, :], rstd5[:, :], 1.0 / D, EPS, ALU.mult, ALU.add).then_inc(var_made, 1)
                            dve.wait_ge(std_made, half_no(i, p // 2, h) + 1)
                            hop(nc.vector.reciprocal(rstd5[:, :], std5[:, :]))
                            hop(nc.vector.scalar_tensor_tensor(f, cent[:, :, :], 0.0, bcast(rstd5), ALU.max, ALU.mult))
                        if p == 3:
                            hop(nc.vector.tensor_scalar(f, tmp[:, :, :], 0.0, None, ALU.max))
                        if p == 4:
                            hop(nc.vector.tensor_tensor(xt, xt, tmp[:, :, :], ALU.add))
                        dve.sem_inc(feats_made, 1)
                        if p < CONVS:
                            dve.wait_ge(prods_made, n + 3)
                            nc.vector.tensor_tensor(
                                root[:, th, :], ps_r[h][:, 0:H * D].rearrange("p (t d) -> p t d", d=D),
                                bias[p][:, :].rearrange("p (a d) -> p a d", a=1).to_broadcast([P, H, D]),
                                ALU.add).then_inc(roots_made, 1)
                        if dense_out:
                            q = p - 2
                            r = resid[:, h, :].rearrange("p (t d) -> p t d", d=D)
                            dve.wait_ge(part1_made, half_no(i, q, h) + 1)
                            nc.vector.tensor_tensor(r, ps_m[h][:, 0:H * D].rearrange("p (t d) -> p t d", d=D),
                                                    hparts[q][:, th, 0:D], ALU.subtract).then_inc(resid_made, 1)
                            dve.sem_inc(prods_taken, 1)
                            dve.wait_ge(resid_made, half_no(i, q, h) + 1)
                            dve.wait_ge(part2_made, half_no(i, q, h) + 1)
                            nc.vector.tensor_tensor(hparts[q][:, th, 2 * D:3 * D], r, hparts[q][:, th, D:2 * D],
                                                    ALU.subtract).then_inc(parts_made, 1)
                    assert seen[0] == 2 * per, (p, seen[0])
                steps[0] = base + 2 * per * NTURNS

            def edge_turn(i, c, half):
                if c == 0:
                    K = GPI * CPG
                    dve.wait_ge(hot_used, i + 1)
                    nc.vector.tensor_tensor(
                        hot_lo[:, :, :],
                        lo_b[:, ds(i * K, K)].rearrange("p (k a) -> p k a", a=1).to_broadcast([P, K, P]),
                        iota_b[:, :].rearrange("p (a m) -> p a m", a=1).to_broadcast([P, K, P]), ALU.is_equal)
                    nc.vector.tensor_tensor(
                        hot_hi[:, :, :],
                        hi_b[:, ds(i * K, K)].rearrange("p (k a) -> p k a", a=1).to_broadcast([P, K, NT]),
                        iota_b[:, 0:NT].rearrange("p (a m) -> p a m", a=1).to_broadcast([P, K, NT]),
                        ALU.is_equal).then_inc(hot_made, 1)
                for g in range(GPI):
                    n = group_no(i, c, g)
                    if half is not None:
                        for w in (2 * g, 2 * g + 1):
                            dve.wait_ge(wins_made, i * WPT + w + 1)
                            for r in range(WCH):
                                col = i * (WPT * WCH) + w * WCH + r
                                nc.vector.tensor_scalar(win_lo[:, w % 2, r, :], iota_k[:, 0:P], loT[:, ds(col, 1)],
                                                        None, ALU.is_equal)
                                last = nc.vector.tensor_scalar(win_key[:, w % 2, r, :], iota_k[:, :],
                                                               keyT[:, ds(col, 1)], None, ALU.is_equal)
                            last.then_inc(wins_hot, 1)
                    dve.wait_ge(mask_in[g], (i + c * TURNS + 1) * 16)
                    dve.wait_ge(msgs_made, n + GPI + 1)
                    dve.wait_ge(back_made, n + 1)
                    dve.wait_ge(scan_done, n + GPI)
                    nc.vector.tensor_tensor_scan(
                        scan[:, g, :], mask[:, g, :], ps_msg[g % 2][0:D, :], scan[:, (g - 1) % GPI, GROUP - 1:GROUP],
                        ALU.add if c in MAXC else ALU.mult,
                        ALU.max if c in MAXC else ALU.add).then_inc(scan_done, 1)

            def edge_loop(c):
                with dve.Fori(0, TURNS) as i:
                    edge_turn(i, c, None)

            def edge_loop_slabs(c):
                with dve.Fori(0, NT) as j:
                    for half in range(2):
                        edge_turn(j * 2 + half, c, half)
                edge_turn(2 * NT, c, None)

            dve.sem_inc(scan_done, GPI)
            dve.sem_inc(featT_copied, 1)
            dve.sem_inc(back_copied, 2)
            dve.sem_inc(prods_taken, 2)
            dve.sem_inc(roots_made, 2)
            dve.sem_inc(wins_copied, 2)
            dve.sem_inc(dense_used, 2)
            dve.wait_ge(edges_in, 64)
            link(nc.vector.tensor_tensor(line[:, :].bitcast(fp32), line[:, :], prev[:, :], ALU.not_equal))
            nc.vector.tensor_scalar(mask_max[:, :], line[:, :].bitcast(fp32), -BIG, None, ALU.mult)
            nc.vector.tensor_scalar(mask_sum[:, :], line[:, :].bitcast(fp32), -1.0, 1.0, ALU.mult, ALU.add).then_inc(masks_made, 1)
            dve.wait_ge(nodes_in, 32)
            dve.wait_ge(weights_in, 16 * W_DMAS)
            dve.wait_ge(pool_const, 2)
            node_pass(0, False, False)
            dve.wait_ge(masks_made, 1)
            link(nc.vector.tensor_scalar(prev[:, :], dst_i[:, :], 7, None, ALU.logical_shift_right))
            nc.vector.tensor_copy(hi_b[:, :], prev[:, :])
            link(nc.vector.tensor_scalar(line[:, :], dst_i[:, :], P - 1, None, ALU.bitwise_and))
            link(nc.vector.tensor_copy(lo_b[:, :], line[:, :]))
            nc.vector.tensor_copy(iota_k[:, :], iota_i[:, :])
            link(nc.vector.tensor_copy(iota_b[:, :], iota_i[:, 0:P]))
            edge_loop(0)

            tot, pre, endf, nonzero = (cnt[k] for k in ("tot", "pre", "endf", "nonzero"))
            dve.wait_ge(deg_made, 1)
            nc.vector.tensor_copy(deg[:, :], ps_deg[:, 0:NT]).then_inc(deg_copied, 1)
            dve.wait_ge(cum_made, 1)
            link(nc.vector.tensor_copy(tot[:, :], ps_cum[:, NT:2 * NT]))
            link(nc.vector.tensor_tensor_scan(pre[:, :], ones[:, 0:NT], tot[:, :], 0.0, ALU.mult, ALU.add))
            link(nc.vector.tensor_tensor(pre[:, :], pre[:, :], tot[:, :], ALU.subtract))
            link(nc.vector.tensor_tensor(endf[:, :], ps_cum[:, 0:NT], pre[:, :], ALU.add))
            link(nc.vector.memset(first_all[:, :], float(EP)))
            link(nc.vector.tensor_tensor(first_all[:, 0:NT], endf[:, :], deg[:, :], ALU.subtract))
            dve.sem_inc(firsts_made, 1)
            link(nc.vector.tensor_scalar(endf[:, :], endf[:, :], -1.0, 0.0, ALU.add, ALU.max))
            link(nc.vector.tensor_copy(end_i[:, :], endf[:, :]))
            link(nc.vector.tensor_scalar(part[:, :], end_i[:, :], 9, 9, ALU.logical_shift_right, ALU.logical_shift_left))
            link(nc.vector.tensor_scalar(part2[:, :], end_i[:, :], P - 1, 2, ALU.bitwise_and, ALU.logical_shift_left))
            link(nc.vector.tensor_tensor(part[:, :], part[:, :], part2[:, :], ALU.bitwise_or))
            link(nc.vector.tensor_scalar(part2[:, :], end_i[:, :], 7, CPG - 1, ALU.logical_shift_right, ALU.bitwise_and))
            link(nc.vector.tensor_tensor(part[:, :], part[:, :], part2[:, :], ALU.bitwise_or))
            link(nc.vector.tensor_scalar(nonzero[:, :], deg[:, :], 0.0, None, ALU.is_gt))
            link(nc.vector.tensor_scalar(endf[:, :], part[:, :], -float(ZROW), None, ALU.add))
            link(nc.vector.tensor_tensor(endf[:, :], endf[:, :], nonzero[:, :], ALU.mult))
            link(nc.vector.tensor_scalar(end_row[:, :], endf[:, :], float(ZROW), None, ALU.add))
            dve.sem_inc(end_rows_made, 1)
            link(nc.vector.tensor_scalar(inv_deg[:, :], deg[:, :], 1.0, None, ALU.max))
            link(nc.vector.reciprocal(inv_deg[:, :], inv_deg[:, :]))
            dve.wait_ge(firsts_turned, 1)
            nc.vector.tensor_copy(first_t[:, :], ps_deg[0:RPT, 0:P]).then_inc(firsts_copied, 1)
            dve.wait_ge(firsts_in, 32)
            link(nc.vector.tensor_copy(row_i[:, :], win_at[:, 0, :, 0]))
            link(nc.vector.tensor_scalar(row_i[:, :], row_i[:, :], 7, None, ALU.logical_shift_right))
            link(nc.vector.tensor_copy(row_f[:, :], row_i[:, :]))
            for r in range(WCH):
                link(nc.vector.tensor_scalar(row_idx[:, :, r], row_f[:, :], float(r), None, ALU.add))
            link(nc.vector.tensor_scalar(lim_f[:, :], row_f[:, :], float(CHUNK), float(WIN_CAP), ALU.mult, ALU.add))
            link(nc.vector.tensor_tensor(bad_w[:, :], win_at[:, 1, :, 0], lim_f[:, :], ALU.is_gt))
            link(nc.vector.tensor_scalar(bad_d[:, :], deg[:, 0:HI], float(DEG_CAP), None, ALU.is_gt))
            dve.sem_inc(rows_known, 1)
            node_pass(1, False, False)
            dve.wait_ge(rows_known, 2)
            link(nc.vector.reduce_sum(bad[:, 0:1], bad_w[:, :], AX.X))
            link(nc.vector.reduce_sum(bad[:, 1:2], bad_d[:, :], AX.X))
            link(nc.vector.tensor_tensor(bad[:, 0:1], bad[:, 0:1], bad[:, 1:2], ALU.add))
            dve.sem_inc(bad_made, 1)
            dve.wait_ge(bad_summed, 1)
            nc.vector.tensor_scalar(ok_i[:, :], ps_cum[0:1, 0:1], 0.0, None, ALU.is_equal).then_inc(ok_known, 1)
            for b in range(WB):
                s_part, d_part = krow[:, :, 0:CHUNK], krow[:, :, CHUNK:2 * CHUNK]
                dve.wait_ge(krow_in, 16 * WCH * (b + 1))
                if b >= 1:
                    dve.wait_ge(keys_turned, b)
                link(nc.vector.tensor_tensor(k_loc[:, :, :], d_part,
                                             win_node[:, b:b + 1].rearrange("p (a c) -> p a c", a=1).to_broadcast([P, WCH, CHUNK]),
                                             ALU.subtract))
                link(nc.vector.tensor_scalar(k_a[:, :, :], k_loc[:, :, :], -WIN, None, ALU.bitwise_and))
                link(nc.vector.tensor_scalar(k_v[:, :, :], k_a[:, :, :], 0.0, None, ALU.is_equal))
                link(nc.vector.tensor_scalar(k_a[:, :, :], s_part, 7, 3, ALU.logical_shift_right, ALU.logical_shift_left))
                link(nc.vector.tensor_tensor(k_key[:, :, :], k_a[:, :, :], k_loc[:, :, :], ALU.add))
                link(nc.vector.scalar_tensor_tensor(k_key[:, :, :], k_key[:, :, :], 1.0, k_v[:, :, :], ALU.add, ALU.mult))
                link(nc.vector.tensor_scalar(k_key[:, :, :], k_key[:, :, :], -1.0, None, ALU.add))
                link(nc.vector.tensor_scalar(k_a[:, :, :], s_part, P - 1, None, ALU.bitwise_and))
                dve.sem_inc(krow_used, 1)
                link(nc.vector.tensor_copy(k_lo[:, :, :], k_a[:, :, :]))
                dve.sem_inc(keys_made, 1)
            dve.wait_ge(keys_copied, WB)
            edge_loop_slabs(1)
            ok = dve.value_load(ok_i[0:1, 0:1])
            at = steps[0]
            with dve.If(ok):
                node_pass(2, False, True)
                node_pass(3, True, True)
                node_pass(4, True, False)
                dve.sem_inc(out_made, 1)
            with dve.Else():
                steps[0] = at
                node_pass(2, False, False)
                edge_loop(2)
                node_pass(3, False, False)
                edge_loop(3)
                node_pass(4, False, False)
                dve.sem_inc(out_made, 1)
            dve.wait_ge(out_made, 1)


_INS = ["x", "src_t", "dst_t", "dst_line", "edges_packed", "attr_t",
        "L0_gnn_W1_msg", "L0_gnn_W1_edge", "L0_gnn_W1_root", "L0_gnn_b1",
        "L0_gnn_W2_msg", "L0_gnn_W2_edge", "L0_gnn_W2_root", "L0_gnn_b2",
        "L1_gnn_W_self1", "L1_gnn_W_neigh1", "L1_gnn_b1",
        "L1_gnn_W_self2", "L1_gnn_W_neigh2", "L1_gnn_b2"]


def kernel(**inputs):
    import numpy as np
    import concourse.bacc as _bacc
    from concourse import mybir as _mybir
    from concourse.bass_utils import run_bass_kernel_spmd as _run

    a = {k: np.asarray(v) for k, v in inputs.items()}
    src = np.concatenate([a["src"], np.zeros(EP - E, a["src"].dtype)])
    dst = np.concatenate([a["dst"], np.full(EP - E, PADN, a["dst"].dtype)])
    a["src_t"] = src.reshape(CHUNKS, P).T
    a["dst_t"] = dst.reshape(CHUNKS, P).T
    a["dst_line"] = np.concatenate([np.full(1, -1, dst.dtype), dst])
    more = WCH * CHUNK
    both = [np.concatenate([v, np.full(more, PADN, v.dtype)]).reshape(EROWS, CHUNK) for v in (src, dst)]
    a["edges_packed"] = np.concatenate(both, axis=1)
    attr = np.concatenate([a["edge_attr_32"], np.zeros((EP - E, DA), a["edge_attr_32"].dtype)])
    a["attr_t"] = attr.reshape(TURNS, GPI, GROUP, DA).transpose(0, 1, 3, 2).reshape(TURNS * P, GROUP)

    nc = _bacc.Bacc("TRN2", target_bir_lowering=False, num_devices=1)
    arrays, args = {}, []
    for name in _INS:
        v = np.ascontiguousarray(a[name])
        arrays[f"in_{name}_dram"] = v
        args.append(nc.dram_tensor(f"in_{name}_dram", v.shape, _mybir.dt.from_np(v.dtype), kind="ExternalInput").ap())
    args.append(nc.dram_tensor("out_0_dram", (N, D), _mybir.dt.float32, kind="ExternalOutput").ap())
    gnn_kernel(nc, *args)
    r = _run(nc, [arrays], core_ids=[0])
    return r.results[0]["out_0_dram"]
```

```python
import concourse.bass as bass
from concourse import mybir
from contextlib import ExitStack


N = 6250
D = 96
DA = 32
E = 206250
P = 128
CHUNK = P
CPG = 4
GROUP = CPG * CHUNK
GPI = 4
TURN = GPI * GROUP
TURNS = -(-E // TURN)
EP = TURNS * TURN
CHUNKS = EP // CHUNK
GROUPS = EP // GROUP
B = 10
H = B // 2
NT = -(-N // (B * P)) * B
NTURNS = NT // B
HALVES = NT // H
FULL = N // P
REST = N - FULL * P
HI = FULL + 1
PADN = NT * P - 1
ZROW = EP
BIG = 3.3895313892515355e38
EPS = 1e-5
CONVS = 4
MAXC = (0, 1)
WIN = 8
WCH = 4
WIN_CAP = WCH * CHUNK
KEYS = HI * WIN
WB = 7
NWIN = -(-N // WIN)
KB = 4
KB_STEP = WB - KB
CSLABS = NT // 2
DEG_CAP = 256
SLABS = 5
FREE_SLABS = 2
PARTS = 3
EROWS = CHUNKS + WCH


def gnn_kernel(nc: bass.Bass, x, src_t, dst_t, dst_line, edges_packed, attr_t,
               w_msg1, w_edge1, w_root1, b1, w_msg2, w_edge2, w_root2, b2,
               s_self1, s_neigh1, sb1, s_self2, s_neigh2, sb2, out):
    fp32 = mybir.dt.float32
    bf16 = mybir.dt.bfloat16
    fp16 = mybir.dt.float16
    i32 = mybir.dt.int32
    ALU = mybir.AluOpType
    ACT = mybir.ActivationFunctionType
    AX = mybir.AxisListType
    ds = bass.ds

    table = nc.dram_tensor("table", (NT * P, D), fp32, kind="Internal").ap()
    scanned_rows = nc.dram_tensor("scanned_rows", (EP + 7, D), fp32, kind="Internal").ap()
    masks = nc.dram_tensor("masks", (2, EP), bf16, kind="Internal").ap()
    slabs = nc.dram_tensor("slabs", (NT, P, HI * P), bf16, kind="Internal").ap()

    ctx = ExitStack()
    with ctx:
        def sb(name, shape, dt=fp32, scope=ctx):
            return scope.enter_context(nc.sbuf_tensor(name, shape, dt))

        def sem(name):
            return ctx.enter_context(nc.semaphore(name))

        ident = sb("ident", [P, P])
        tri = sb("tri", [P, P])
        ones = sb("ones", [P, P])
        ident16 = sb("ident16", [P, P], fp16)
        zbf = sb("zbf", [P, P], bf16)
        zrow = sb("zrow", [1, D])
        epsc = sb("epsc", [P, 1])
        win_node = sb("win_node", [P, WB], i32)
        win_node_f = sb("win_node_f", [P, WB])
        row_first = sb("row_first", [P, CHUNKS])
        w_cat = [sb(f"w_cat{c}", [D + 1, 2 * D]) for c in range(CONVS)]
        w_edge = [sb(f"w_edge{c}", [P, GPI, D]) for c in MAXC]
        iota_k = sb("iota_k", [P, KEYS + 1], fp16)
        src_i = sb("src_i", [P, CHUNKS + GPI * CPG], i32)
        xs = sb("xs", [P, NT, D])
        root = sb("root", [P, NT, D])
        deg = sb("deg", [P, NT])
        inv_deg = sb("inv_deg", [P, NT])
        end_row = sb("end_row", [P, NT], i32)
        end_idx = sb("end_idx", [P, B], i32)
        row_at = sb("row_at", [P, 2, WB])
        row_idx = sb("row_idx", [P, WB, WCH], i32)
        agg = sb("agg", [P, B, D])
        feat = sb("feat", [P, B, D + 1])
        tmp = sb("tmp", [P, H, D])
        cent = sb("cent", [P, H, D])
        stats = sb("stats", [P, H, 6])
        mv = sb("mv", [P, 2, H, 2])
        std = sb("std", [P, 2, H])
        rstd = sb("rstd", [P, 2, H])
        shift = sb("shift", [P, 2, H])
        featT = sb("featT", [D + 1, 2, H * P])
        msg = sb("msg", [P, B, D])
        row_i = row_first[:, :].bitcast(i32)
        ok_i = sb("ok_i", [1, 1], i32)
        cnt = {n: sb(n, [P, NT]) for n in ("tot", "pre", "endf", "nonzero")}
        end_i = sb("end_i", [P, NT], i32)
        part = sb("part", [P, NT], i32)
        part2 = sb("part2", [P, NT], i32)
        early = ExitStack()
        with early:
            bad = sb("bad", [P, 2], scope=early)
            bad_w = sb("bad_w", [P, WB], scope=early)
            bad_d = sb("bad_d", [P, HI], scope=early)
            krow = sb("krow", [P, KB, WCH, 2 * CHUNK], i32, early)
            k_loc = sb("k_loc", [P, WCH, CHUNK], i32, early)
            k_s = sb("k_s", [P, WCH, CHUNK], i32, early)
            k_key = sb("k_key", [P, WCH, CHUNK], fp16, early)
            k_lo = sb("k_lo", [P, WCH, CHUNK], fp16, early)
            lists = ExitStack()
            with lists:
                line = sb("line", [P, CHUNKS + 1], i32, lists)
                scratch_i = sb("scratch_i", [P, CHUNKS], i32, lists)
                hi_b = sb("hi_b", [P, CHUNKS], bf16, lists)
                lo_b = sb("lo_b", [P, CHUNKS], bf16, lists)
                mask_max = sb("mask_max", [P, CHUNKS], bf16, lists)
                mask_sum = sb("mask_sum", [P, CHUNKS], bf16, lists)
                row_flag = sb("row_flag", [P, CHUNKS], bf16, lists)
                iota_i = k_loc[:, :, :].rearrange("p r e -> p (r e)")[:, 0:KEYS + 1]
                iota_b = sb("iota_b", [P, P], bf16, lists)
        hparts = [sb(f"hparts{j}", [P, NT, PARTS * D], bf16) for j in range(2)]
        kept = hparts[1][:, :, :].bitcast(fp32)[:, :, 0:D]
        sparse = ExitStack()
        with sparse:
            idx = sb("idx", [P, GPI, CPG], i32, sparse)
            rows = sb("rows", [P, GPI, CPG, D], scope=sparse)
            attr = sb("attr", [P, GROUP], scope=sparse)
            mask = sb("mask", [D, GPI, GROUP], bf16, sparse)
            scan = sb("scan", [D, GPI, GROUP], scope=sparse)
            keyT = sb("keyT", [P, KB * P * WCH], scope=sparse)
            loT = sb("loT", [P, KB * P * WCH], scope=sparse)
            turns_only = ExitStack()
            with turns_only:
                back = sb("back", [P, GPI, CPG * D], scope=turns_only)
                hot_lo = sb("hot_lo", [P, GPI * CPG, P], bf16, turns_only)
                hot_hi = sb("hot_hi", [P, GPI * CPG, NT], bf16, turns_only)
                win_lo = sb("win_lo", [P, 2, WCH, P], bf16, turns_only)
                win_key = sb("win_key", [P, 2, WCH, KEYS], bf16, turns_only)
                new_slab = sb("new_slab", [P, HI, P], bf16, turns_only)
            featT_all = sb("featT_all", [D + 1, NT, P], scope=sparse)
        slab = sb("slab", [P, SLABS, HI, P], bf16)

        psum = ctx.enter_context(nc.psum_tensor("psum", [P, 8, GROUP], fp32))
        ps_msg = [psum[:, j, :] for j in (0, 1)]
        ps_back = [psum[:, j, :] for j in (2, 3)]
        ps_win = [psum[:, j, :] for j in (4, 5)]
        ps_deg = psum[:, 6, :]
        ps_cum = psum[:, 7, :]
        ps_turned = [psum[:, j:j + 2, :].rearrange("p a b -> p (a b)") for j in (0, 4)]
        ps_m = [psum[:, j, :] for j in (2, 3)]
        ps_r = [psum[:, j, :] for j in (6, 7)]

        weights_in = sem("weights_in")
        edges_in = sem("edges_in")
        nodes_in = sem("nodes_in")
        zeroed = sem("zeroed")
        masks_made = sem("masks_made")
        masks_stored = sem("masks_stored")
        pool_const = sem("pool_const")
        dve_step = sem("dve_step")
        pool_passed = sem("pool_passed")
        rows_in = sem("rows_in")
        dve_passed = sem("dve_passed")
        act_passed = sem("act_passed")
        hot_made = sem("hot_made")
        hot_used = sem("hot_used")
        deg_made = sem("deg_made")
        deg_copied = sem("deg_copied")
        cum_made = sem("cum_made")
        end_rows_made = sem("end_rows_made")
        rows_known = sem("rows_known")
        krow_in = [sem(f"krow_in{b}") for b in range(KB)]
        krow_used = sem("krow_used")
        keys_made = sem("keys_made")
        keys_turned = sem("keys_turned")
        keys_copied = sem("keys_copied")
        bad_made = sem("bad_made")
        bad_summed = sem("bad_summed")
        ok_known = sem("ok_known")
        wins_hot = sem("wins_hot")
        wins_made = sem("wins_made")
        wins_copied = sem("wins_copied")
        slab_stored = sem("slab_stored")
        idx_staged = sem("idx_staged")
        gathered = [sem(f"gathered{g}") for g in range(GPI)]
        attr_in = sem("attr_in")
        mask_in = [sem(f"mask_in{g}") for g in range(GPI)]
        msgs_made = sem("msgs_made")
        scan_done = sem("scan_done")
        back_made = sem("back_made")
        back_copied = sem("back_copied")
        back_stored = [sem(f"back_stored{g}") for g in range(GPI)]
        end_staged = sem("end_staged")
        agg_in = [sem(f"agg_in{h}") for h in range(2)]
        feats_made = sem("feats_made")
        feats_turned = sem("feats_turned")
        featT_copied = sem("featT_copied")
        prods_made = sem("prods_made")
        prods_taken = sem("prods_taken")
        root_prods_made = sem("root_prods_made")
        roots_made = sem("roots_made")
        first_weights_in = sem("first_weights_in")
        table_stored = [sem(f"table_stored{h}") for h in range(2)]
        var_made = sem("var_made")
        std_made = sem("std_made")
        norm_made = sem("norm_made")
        resid_made = sem("resid_made")
        part2_made = sem("part2_made")
        kept_less = sem("kept_less")
        kept_part2 = sem("kept_part2")
        parts_made = sem("parts_made")
        agg_used = sem("agg_used")
        nexts_in = sem("nexts_in")
        lines_in = sem("lines_in")
        slab_in = [sem(f"slab_in{j}") for j in range(SLABS)]
        dense_made = sem("dense_made")
        dense_used = sem("dense_used")
        out_made = sem("out_made")
        out_stored = sem("out_stored")

        block = ctx.enter_context(nc.Block())

        W_DMAS = 3 * (CONVS - 1) + GPI * len(MAXC)

        def half_no(i, p, h):
            return i * 2 + (p * HALVES + h)

        def group_no(i, c, g):
            return i * GPI + (c * GROUPS + g)

        LAST_ROOTS = [(n // 2, n % 2) for n in range(HALVES - KB, HALVES)]

        def win_no(i, c, w):
            return i * GPI + (c * CSLABS * 4 * GPI + w)

        @block.sync
        def _(sp):
            def store_table(c):
                with sp.Fori(0, NTURNS) as i:
                    for h in range(2):
                        sp.wait_ge(prods_taken, half_no(i, c, h) + 3)
                        sp.dma_start(
                            table[ds(i * (B * P) + h * H * P, H * P), :].rearrange("(t p) d -> p t d", p=P),
                            msg[:, h * H:(h + 1) * H, :]).then_inc(table_stored[h], 16)

            def edge_loads(c):
                with sp.Fori(0, TURNS) as i:
                    for g in range(GPI):
                        if g == 0 and c in MAXC:
                            sp.wait_ge(msgs_made, group_no(i, c, GPI))
                            sp.dma_start(attr[:, :], attr_t[ds(i * P, P), :]).then_inc(attr_in, 16)
                        sp.wait_ge(scan_done, group_no(i, c, g + 1))
                        m = masks[0 if c in MAXC else 1, ds(i * TURN + g * GROUP, GROUP)]
                        sp.dma_start(mask[:, g, :], m.rearrange("(a e) -> a e", a=1).to_broadcast([D, GROUP])).then_inc(mask_in[g], 16)

            def slab_load(i, c, s):
                t = i * B + ((c - 2) * NT + s)
                sp.wait_ge(dense_made, t + 1)
                sp.dma_start(slab[:, s % SLABS].rearrange("p k d -> p (k d)"),
                             slabs[ds(i * B + s, 1), :, :].rearrange("a p n -> p (a n)")).then_inc(slab_in[s % SLABS], 16)

            def weight_loads(c, wm, wr, b, landed):
                sp.dma_start(w_cat[c][0:D, 0:D], wm).then_inc(landed, 16)
                sp.dma_start(w_cat[c][0:D, D:2 * D], wr).then_inc(landed, 16)
                sp.dma_start(w_cat[c][D:D + 1, D:2 * D], b.rearrange("(a d) -> a d", a=1)).then_inc(landed, 16)

            sp.dma_start(line[:, :], dst_line).then_inc(lines_in, 16)
            sp.dma_start(xs[:, 0:FULL, :], x[0:FULL * P, :].rearrange("(t p) d -> p t d", p=P)).then_inc(nodes_in, 16)
            sp.wait_ge(zeroed, 1)
            sp.dma_start(xs[0:REST, FULL, :], x[FULL * P:N, :]).then_inc(nodes_in, 16)
            sp.dma_start(row_i, dst_t[0:1, :].to_broadcast([P, CHUNKS])).then_inc(rows_in, 16)
            weight_loads(0, w_msg1, w_root1, b1, first_weights_in)
            sp.dma_start(src_i[:, 0:CHUNKS], src_t).then_inc(edges_in, 16)
            for c, (wm, wr, b) in enumerate([(w_msg2, w_root2, b2), (s_neigh1, s_self1, sb1), (s_neigh2, s_self2, sb2)]):
                weight_loads(c + 1, wm, wr, b, weights_in)
            for c, we in enumerate([w_edge1, w_edge2]):
                for g in range(GPI):
                    sp.dma_start(w_edge[c][DA * g:DA * g + DA, g, :], we).then_inc(weights_in, 16)
            for j, stored in enumerate(back_stored + table_stored + [slab_stored]):
                sp.dma_start(scanned_rows[ZROW + j:ZROW + j + 1, :], zrow[0:1, :]).then_inc(stored, 16)
            sp.wait_ge(masks_made, 1)
            sp.dma_start(masks[0, :].rearrange("(p c) -> p c", p=P), mask_max[:, :]).then_inc(masks_stored, 16)
            sp.dma_start(masks[1, :].rearrange("(p c) -> p c", p=P), mask_sum[:, :]).then_inc(masks_stored, 16)
            store_table(0)
            sp.wait_ge(rows_known, 1)
            sp.dma_start(row_at[0:P - 1, 1, :], row_at[1:P, 0, :]).then_inc(nexts_in, 16)
            sp.dma_start(row_at[P - 1:P, 1, 0:WB - 1], row_at[0:1, 0, 1:WB]).then_inc(nexts_in, 16)
            sp.wait_ge(masks_stored, 32)
            edge_loads(0)
            store_table(1)
            edge_loads(1)
            sp.wait_ge(ok_known, 1)
            ok = sp.value_load(ok_i[0:1, 0:1])
            with sp.If(ok):
                sp.wait_ge(slab_stored, 16 * (NT + 1))
                sp.wait_ge(feats_made, 3 * HALVES)
                for s in range(FREE_SLABS):
                    slab_load(0, 2, s)
                sp.wait_ge(roots_made, 3 * HALVES + 2)
                for s in range(FREE_SLABS, B):
                    slab_load(0, 2, s)
                for c, begin in ((2, 1), (3, 0)):
                    with sp.Fori(begin, NTURNS) as i:
                        for s in range(B):
                            slab_load(i, c, s)
            with sp.Else():
                for c in (2, 3):
                    store_table(c)
                    edge_loads(c)

        @block.gpsimd
        def _(pool):
            def gather_edges(c):
                pool.wait_ge(table_stored[0], 16 * NTURNS * (c + 1) + 16)
                pool.wait_ge(table_stored[1], 16 * NTURNS * (c + 1) + 16)
                with pool.Fori(0, TURNS) as i:
                    for g in range(GPI):
                        n = group_no(i, c, g)
                        pool.wait_ge(idx_staged, n + (c * GPI + 1))
                        pool.wait_ge(msgs_made, n + 1)
                        pool.sem_inc(pool_passed, 1)
                        for k in range(CPG):
                            pool.indirect_dma_start(
                                rows[:, g, k, :], None, table,
                                bass.IndirectOffsetOnAxis(ap=idx[:, g, k:k + 1], axis=0)).then_inc(gathered[g], 16)

            def gather_ends(c):
                for g in range(GPI):
                    pool.wait_ge(back_stored[g], 16 * TURNS * (c + 1) + 16)
                pool.wait_ge(end_rows_made, 1)
                with pool.Fori(0, NTURNS) as i:
                    for h in range(2):
                        pool.wait_ge(agg_used, half_no(i, c, h) + 1)
                        pool.tensor_copy(end_idx[:, h * H:(h + 1) * H], end_row[:, ds(i * B + h * H, H)]).then_inc(end_staged, 1)
                        pool.wait_ge(end_staged, half_no(i, c, h) + 1)
                        pool.sem_inc(pool_passed, 1)
                        for s in range(h * H, (h + 1) * H):
                            pool.indirect_dma_start(
                                agg[:, s, :], None, scanned_rows,
                                bass.IndirectOffsetOnAxis(ap=end_idx[:, s:s + 1], axis=0)).then_inc(agg_in[h], 16)

            def gather_keys(c, blocks):
                for b in blocks:
                    if c == 1:
                        pool.wait_ge(krow_used, b + 1)
                    for r in range(WCH):
                        pool.indirect_dma_start(
                            krow[:, b, r, :], None, edges_packed,
                            bass.IndirectOffsetOnAxis(ap=row_idx[:, c * KB_STEP + b, r:r + 1], axis=0)).then_inc(krow_in[b], 16)

            def reduce_kept():
                with pool.Fori(0, NTURNS - 1) as i:
                    t = ds(i * B, B)
                    pool.wait_ge(prods_taken, half_no(i, 2, 1) + 3)
                    pool.sem_inc(pool_passed, 1)
                    pool.tensor_tensor(kept[:, t, :], kept[:, t, :], hparts[0][:, t, 0:D], ALU.subtract).then_inc(kept_less, 1)

            def split_messages():
                with pool.Fori(0, NTURNS) as i:
                    for h in range(2):
                        m = msg[:, h * H:(h + 1) * H, :]
                        part = [hparts[1][:, ds(i * B + h * H, H), j * D:(j + 1) * D] for j in range(PARTS)]
                        n = half_no(i, 0, h)
                        pool.wait_ge(prods_taken, half_no(i, 3, h) + 3)
                        pool.sem_inc(pool_passed, 1)
                        pool.tensor_tensor(m, m, part[0], ALU.subtract).then_inc(resid_made, 1)
                        pool.wait_ge(resid_made, n + 1)
                        pool.wait_ge(part2_made, n + 1)
                        pool.sem_inc(pool_passed, 1)
                        pool.tensor_tensor(part[2], m, part[1], ALU.subtract).then_inc(parts_made, 1)

            pool.memset(xs[:, FULL:NT, :], 0.0)
            for c in range(CONVS):
                pool.memset(w_cat[c][:, :], 0.0)
            pool.memset(feat[:, :, :], 1.0)
            pool.memset(row_at[:, :, :], 0.0)
            pool.memset(epsc[:, :], EPS)
            pool.memset(src_i[:, CHUNKS:], 0)
            pool.memset(zrow[:, :], 0.0)
            pool.memset(w_edge[0][:, :, :], 0.0)
            pool.memset(w_edge[1][:, :, :], 0.0)
            pool.memset(scan[:, :, :], 0.0).then_inc(zeroed, 1)
            pool.memset(zbf[:, :], 0.0)
            pool.memset(ones[:, :], 1.0)
            pool.memset(ident[:, :], 0.0).then_inc(pool_const, 1)
            pool.wait_ge(pool_const, 1)
            pool.affine_select(out=ident[:, :], in_=ident[:, :], compare_op=ALU.not_equal, fill=1.0,
                               base=0, pattern=[[-1, P]], channel_multiplier=1)
            pool.affine_select(out=tri[:, :], in_=ones[:, :], compare_op=ALU.is_ge, fill=0.0,
                               base=0, pattern=[[1, P]], channel_multiplier=-1)
            pool.iota(win_node[:, :], pattern=[[P * WIN, WB]], base=0, channel_multiplier=WIN)
            pool.iota(iota_i, pattern=[[1, KEYS + 1]], base=0, channel_multiplier=0).then_inc(pool_const, 1)
            pool.wait_ge(rows_known, 1)
            gather_keys(0, range(KB))
            gather_edges(0)
            gather_keys(1, range(KB // 2))
            gather_ends(0)
            pool.wait_ge(rows_known, 2)
            pool.affine_select(out=bad_w[:, :], in_=bad_w[:, :], compare_op=ALU.is_ge, fill=0.0,
                               base=NWIN - 1, pattern=[[-P, WB]], channel_multiplier=-1).then_inc(rows_known, 1)
            gather_keys(1, range(KB // 2, KB))
            gather_edges(1)
            gather_ends(1)
            pool.wait_ge(ok_known, 1)
            ok = pool.value_load(ok_i[0:1, 0:1])
            with pool.If(ok):
                reduce_kept()
                split_messages()
            with pool.Else():
                for c in (2, 3):
                    gather_edges(c)
                    gather_ends(c)

        @block.scalar
        def _(act):
            def copy_turned(i, p, h, banks):
                n = half_no(i, p, h)
                act.wait_ge(feats_turned, n + 3)
                act.sem_inc(act_passed, 1)
                t = i * B + h * H
                nc.scalar.copy(featT_all[:, ds(t, H - 1), :],
                               banks[0:D + 1, 0:GROUP].rearrange("p (t n) -> p t n", n=P))
                nc.scalar.copy(featT_all[:, ds(t + (H - 1), 1), :],
                               banks[0:D + 1, GROUP:H * P].rearrange("p (t n) -> p t n", n=P)).then_inc(featT_copied, 1)

            def copy_turned_dense(i, p, h, banks):
                n = half_no(i, p, h)
                act.wait_ge(feats_turned, n + 3)
                act.wait_ge(root_prods_made, n + 1)
                for o in (slice(0, GROUP), slice(GROUP, H * P)):
                    last = nc.scalar.copy(featT[:, h, o], banks[0:D + 1, o])
                last.then_inc(featT_copied, 1)

            def copy_products(i, p, h, form):
                n = half_no(i, p, h)
                th = ds(i * B + h * H, H)
                m = ps_m[h][:, 0:H * D].rearrange("p (t d) -> p t d", d=D)
                slot = msg[:, h * H:(h + 1) * H, :]
                act.wait_ge(prods_made, n + 3)
                if form == "stored":
                    act.wait_ge(table_stored[h], (i + p * NTURNS) * 16 + 16)
                    nc.scalar.copy(slot, m).then_inc(prods_taken, 1)
                if form == "kept":
                    act.sem_inc(act_passed, 1)
                    nc.scalar.copy(kept[:, th, :], m)
                    nc.scalar.copy(hparts[0][:, th, 0:D], m).then_inc(prods_taken, 1)
                if form == "split":
                    act.wait_ge(parts_made, half_no(i, 0, h) + (NTURNS - 1))
                    act.sem_inc(act_passed, 1)
                    nc.scalar.copy(hparts[1][:, th, 0:D], m)
                    nc.scalar.copy(slot, m).then_inc(prods_taken, 1)

            def copy_root(i, p, h):
                act.wait_ge(root_prods_made, half_no(i, p, h) + 3)
                act.sem_inc(act_passed, 1)
                nc.scalar.copy(root[:, ds(i * B + h * H, H), :],
                               ps_r[h][:, 0:H * D].rearrange("p (t d) -> p t d", d=D)).then_inc(roots_made, 1)

            def copy_last_roots(p, with_keys=False):
                for b in range(KB):
                    copy_root(LAST_ROOTS[b][0], p, LAST_ROOTS[b][1])
                    if with_keys:
                        copy_keys(p, b)

            def deviation(i, p, h):
                act.wait_ge(var_made, half_no(i, p // 2, h) + 1)
                nc.scalar.activation(std[:, h, :], mv[:, h, :, 1], ACT.Sqrt, bias=epsc[:, 0:1]).then_inc(std_made, 1)

            def normalize(i, p, h):
                act.wait_ge(norm_made, half_no(i, p // 2, h) + 1)
                act.wait_ge(feats_turned, half_no(i, p, h) + 1)
                act.sem_inc(act_passed, 1)
                for s in range(H):
                    last = nc.scalar.activation(
                        feat[:, h * H + s, 0:D], xs[:, ds(i * B + (h * H + s), 1), :].rearrange("p t d -> p (t d)"),
                        ACT.Relu, bias=shift[:, h, s:s + 1], scale=rstd[:, h, s:s + 1])
                last.then_inc(feats_made, 1)

            def node_pass(p, form):
                def step(turned, normed, taken, rooted=None):
                    if normed and p in (0, 2):
                        deviation(normed[0], p, normed[1])
                    copy_turned(turned[0], p, turned[1], ps_turned[turned[1]])
                    if normed and p in (0, 2):
                        normalize(normed[0], p, normed[1])
                    if taken:
                        copy_products(taken[0], p, taken[1], form)
                    if rooted:
                        copy_root(rooted[0], p, rooted[1])

                if p in (0, 2):
                    deviation(0, p, 0)
                    normalize(0, p, 0)
                step((0, 0), (0, 1), None)
                step((0, 1), (1, 0), (0, 0))
                step((1, 0), (1, 1), (0, 1), (0, 0))
                with act.Fori(1, NTURNS - 2) as i:
                    step((i, 1), (i + 1, 0), (i, 0), (i - 1, 1))
                    step((i + 1, 0), (i + 1, 1), (i, 1), (i, 0))
                i = NTURNS - 2
                step((i, 1), (i + 1, 0), (i, 0), (i - 1, 1))
                step((i + 1, 0), (i + 1, 1), (i, 1))
                step((NTURNS - 1, 1), None, (NTURNS - 1, 0))
                copy_products(NTURNS - 1, p, 1, form)

            def dense_pass(p):
                with act.Fori(0, NTURNS) as i:
                    for h in range(2):
                        copy_turned_dense(i, p, h, ps_turned[0])
                        copy_products(i, p, h, "split")
                        copy_root(i, p, h)
                        act.wait_ge(resid_made, half_no(i, 0, h) + 1)
                        act.sem_inc(act_passed, 1)
                        nc.scalar.copy(hparts[1][:, ds(i * B + h * H, H), D:2 * D],
                                       msg[:, h * H:(h + 1) * H, :]).then_inc(part2_made, 1)

            def store_result():
                with act.Fori(0, NTURNS - 1) as i:
                    for h in range(2):
                        act.wait_ge(out_made, i * 2 + (h + 1))
                        act.dma_start(out[ds(i * (B * P) + h * H * P, H * P), :].rearrange("(t p) d -> p t d", p=P),
                                      xs[:, ds(i * B + h * H, H), :]).then_inc(out_stored, 16)
                last = (NTURNS - 1) * B
                act.wait_ge(out_made, HALVES - 1)
                act.dma_start(out[last * P:(last + H) * P, :].rearrange("(t p) d -> p t d", p=P),
                              xs[:, last:last + H, :]).then_inc(out_stored, 16)
                act.wait_ge(out_made, HALVES)
                act.dma_start(out[(last + H) * P:FULL * P, :].rearrange("(t p) d -> p t d", p=P),
                              xs[:, last + H:FULL, :]).then_inc(out_stored, 16)
                act.dma_start(out[FULL * P:N, :], xs[0:REST, FULL, :]).then_inc(out_stored, 16)
                act.wait_ge(out_stored, 16 * (HALVES + 1))

            def edge_turn(i, c, quarter=None):
                for g in range(GPI):
                    n = group_no(i, c, g)
                    act.wait_ge(msgs_made, n + GPI + 1)
                    nc.scalar.copy(idx[:, g, :], src_i[:, ds(i * (GPI * CPG) + (GPI + g) * CPG, CPG)]).then_inc(idx_staged, 1)
                    if quarter is not None:
                        v = i - 1
                        act.wait_ge(wins_made, win_no(v, c, g) + 3)
                        if (quarter, g) == (0, 0):
                            act.wait_ge(slab_stored, v * 4 + (c * CSLABS + 1) * 16)
                        node = (quarter * GPI + g) * WIN
                        nc.scalar.copy(new_slab[:, :, node:node + WIN],
                                       ps_win[g % 2][:, 0:KEYS].rearrange("p (k d) -> p k d", d=WIN)).then_inc(wins_copied, 1)
                    act.wait_ge(back_made, n + GPI + 1)
                    act.wait_ge(back_stored[g], (i + c * TURNS) * 16 + 16)
                    nc.scalar.copy(back[:, g, :], ps_back[g % 2][:, 0:CPG * D]).then_inc(back_copied, 1)
                    act.wait_ge(back_copied, n + 3)
                    act.dma_start(
                        scanned_rows[ds(i * TURN + g * GROUP, GROUP), :].rearrange("(p k) d -> p (k d)", k=CPG),
                        back[:, g, :]).then_inc(back_stored[g], 16)

            def first_indices(c):
                act.wait_ge(msgs_made, c * GROUPS + GPI)
                for g in range(GPI):
                    nc.scalar.copy(idx[:, g, :], src_i[:, g * CPG:(g + 1) * CPG]).then_inc(idx_staged, 1)

            def edge_loop(c):
                with act.Fori(0, TURNS) as i:
                    edge_turn(i, c)

            def edge_loop_slabs(c):
                edge_turn(0, c)
                with act.Fori(0, CSLABS) as j:
                    for quarter in range(4):
                        edge_turn(j * 4 + (quarter + 1), c, quarter)
                    act.wait_ge(wins_copied, win_no(j * 4, c, 4 * GPI) + 2)
                    act.dma_start(slabs[ds(j + c * CSLABS, 1), :, :].rearrange("a p n -> p (a n)"),
                                  new_slab[:, :, :].rearrange("p k d -> p (k d)")).then_inc(slab_stored, 16)

            def copy_keys(c, b):
                act.wait_ge(keys_turned, c * KB + b + 1)
                for o, bank in ((keyT, 0), (loT, 1)):
                    last = nc.scalar.copy(
                        o[:, b * P * WCH:(b + 1) * P * WCH].rearrange("p (w r) -> p r w", r=WCH),
                        ps_win[bank].rearrange("p (r w) -> p r w", r=WCH))
                last.then_inc(keys_copied, 1)

            node_pass(0, "stored")
            act.wait_ge(edges_in, 16)
            first_indices(0)
            copy_last_roots(0, with_keys=True)
            edge_loop_slabs(0)
            first_indices(1)
            act.wait_ge(slab_stored, (CSLABS + 1) * 16)
            node_pass(1, "stored")
            copy_last_roots(1, with_keys=True)
            edge_loop_slabs(1)
            act.wait_ge(ok_known, 1)
            ok = act.value_load(ok_i[0:1, 0:1])
            with act.If(ok):
                act.wait_ge(slab_stored, (NT + 1) * 16)
                node_pass(2, "kept")
                copy_last_roots(2)
                dense_pass(3)
            with act.Else():
                act.wait_ge(slab_stored, (NT + 1) * 16)
                for c in (2, 3):
                    first_indices(c)
                    node_pass(c, "stored")
                    copy_last_roots(c)
                    edge_loop(c)
            store_result()

        @block.tensor
        def _(pe):
            def turn_half(i, p, h, banks, lag):
                n = half_no(i, p, h)
                pe.wait_ge(feats_made, n + 1)
                pe.wait_ge(featT_copied, n + (3 - lag))
                for s in range(H):
                    last = nc.tensor.transpose(banks[0:D + 1, s * P:(s + 1) * P], feat[:, h * H + s, :], ident[:, :])
                last.then_inc(feats_turned, 1)

            def multiply_half(i, p, h, turned, name, free, made):
                n = half_no(i, p, h)
                ps, w = (ps_m, w_cat[p][:, 0:D]) if name == "msg" else (ps_r, w_cat[p][:, D:2 * D])
                pe.wait_ge(featT_copied, n + 3)
                pe.wait_ge(free, n + 1)
                for s in range(H):
                    last = nc.tensor.matmul(ps[h][:, s * D:(s + 1) * D], turned(i, h, s), w, start=True, stop=True)
                last.then_inc(made, 1)

            def messages_half(i, h, p, turned=None):
                multiply_half(i, p, h, turned or in_all, "msg", prods_taken, prods_made)

            def root_half(i, h, p, turned=None):
                multiply_half(i, p, h, turned or in_all, "root", roots_made, root_prods_made)

            def in_all(i, h, s):
                return featT_all[:, i * B + h * H + s, :]

            def in_ring(i, h, s):
                return featT[:, h, s * P:(s + 1) * P]

            def dense_tile(i, q, s, first=False, begin=0, end=HI, done=True):
                t = i * B + (q * NT + s)
                if begin == 0:
                    pe.wait_ge(slab_in[s % SLABS], (i * (B // SLABS) + (q * (NT // SLABS) + s // SLABS + 1)) * 16)
                    pe.wait_ge(dense_used, t + 1)
                for k in range(begin, end):
                    if first and k % (B, H)[q] == 0:
                        pe.wait_ge(parts_made, q * NTURNS + k // (B, H)[q] + 1)
                    last = nc.tensor.matmul(ps_win[s % 2][:, 0:PARTS * D], slab[:, s % SLABS, k, :],
                                            hparts[q][:, k, :], start=k == 0, stop=done and k == end - 1)
                if done:
                    last.then_inc(dense_made, 1)

            def node_pass(p, with_keys=False):
                def turn(i, h):
                    turn_half(i, p, h, ps_turned[h], 2)

                halves = [(i, h) for i in range(NTURNS) for h in range(2)]
                turn(0, 0)
                for n in range(1, HALVES):
                    turn(*halves[n])
                    messages_half(*halves[n - 1], p)
                    if n >= 2 and halves[n - 2] not in LAST_ROOTS:
                        root_half(*halves[n - 2], p)
                messages_half(*halves[-1], p)
                for b in range(KB):
                    root_half(*LAST_ROOTS[b], p)
                    if with_keys:
                        turn_keys(p, b)
                pe.wait_ge(roots_made, (p + 1) * HALVES + 2)
                if with_keys:
                    pe.wait_ge(keys_copied, (p + 1) * KB)

            def dense_half(i, q, h, begin=0, last=False):
                for s in range(h * H + begin, (h + 1) * H):
                    dense_tile(i, q, s, end=1 if last and (NTURNS - 1) * B + s >= HI else HI)

            def dense_pass(p):
                q = p - 3

                def node_half(i, h):
                    turn_half(i, p, h, ps_turned[0], 1)
                    messages_half(i, h, p, in_ring)
                    root_half(i, h, p, in_ring)

                dense_tile(0, q, 0, True)
                dense_half(0, q, 0, 1)
                with pe.Fori(0, NTURNS - 1) as i:
                    dense_half(i, q, 1)
                    node_half(i, 0)
                    dense_half(i + 1, q, 0)
                    node_half(i, 1)
                dense_half(NTURNS - 1, q, 1, last=True)
                node_half(NTURNS - 1, 0)
                dense_tile(0, q + 1, 0, True, 0, NT - B, False)
                node_half(NTURNS - 1, 1)
                dense_tile(0, q + 1, 1, False, 0, NT - B, False)
                dense_tile(0, q + 1, 0, True, NT - B)
                dense_tile(0, q + 1, 1, False, NT - B)

            def edge_turn(i, c, quarter=None):
                def gather_in(g):
                    n = group_no(i, c, g)
                    bank = ps_msg[g % 2][0:D, :]
                    pe.wait_ge(scan_done, n + 3)
                    if c in MAXC:
                        if g == 0:
                            pe.wait_ge(attr_in, (i + c * TURNS + 1) * 16)
                        nc.tensor.matmul(bank, w_edge[c][:, g, :], attr[:, :], start=True, stop=False)
                    pe.wait_ge(gathered[g], (i + c * TURNS + 1) * (16 * CPG))
                    for k in range(CPG):
                        o = bank[:, k * CHUNK:(k + 1) * CHUNK]
                        if c in MAXC:
                            last = nc.tensor.matmul(o, rows[:, g, k, :], ident[:, :], start=False, stop=k == CPG - 1)
                        else:
                            last = nc.tensor.transpose(o, rows[:, g, k, :], ident[:, :])
                    last.then_inc(msgs_made, 1)

                def scan_out(g):
                    n = group_no(i, c, g)
                    pe.wait_ge(scan_done, n + GPI + 1)
                    pe.wait_ge(back_copied, n + 1)
                    for k in range(CPG):
                        last = nc.tensor.transpose(ps_back[g % 2][:, k * D:(k + 1) * D],
                                                   scan[:, g, k * CHUNK:(k + 1) * CHUNK], ident[0:D, 0:D])
                    last.then_inc(back_made, 1)

                def window(w):
                    v = i - 1
                    pe.wait_ge(wins_hot, win_no(v, c, w) + 1)
                    pe.wait_ge(wins_copied, win_no(v, c, w) + 1)
                    for r in range(WCH):
                        last = nc.tensor.matmul(ps_win[w % 2][:, 0:KEYS], win_lo[:, w % 2, r, :], win_key[:, w % 2, r, :],
                                                start=r == 0, stop=r == WCH - 1)
                    last.then_inc(wins_made, 1)

                if c == 0:
                    pe.wait_ge(hot_made, i + 1)
                    for k in range(GPI * CPG):
                        last = nc.tensor.matmul(ps_deg[:, 0:NT], hot_lo[:, k, :], hot_hi[:, k, :], start=False,
                                                stop=False)
                    last.then_inc(hot_used, 1)
                for g in range(GPI):
                    gather_in(g)
                    if quarter is not None:
                        window(g)
                    if g >= 1:
                        scan_out(g - 1)
                scan_out(GPI - 1)

            def edge_loop(c):
                with pe.Fori(0, TURNS) as i:
                    edge_turn(i, c)

            def edge_loop_slabs(c):
                edge_turn(0, c)
                with pe.Fori(0, CSLABS) as j:
                    for quarter in range(4):
                        edge_turn(j * 4 + (quarter + 1), c, quarter)

            def turn_keys(c, b):
                u = c * KB + b
                pe.wait_ge(keys_made, u + 1)
                if u >= 1:
                    pe.wait_ge(keys_copied, u)
                for bank, k in ((0, k_key), (1, k_lo)):
                    for r in range(WCH):
                        last = nc.tensor.matmul(ps_win[bank][:, r * P:(r + 1) * P], k[:, r, :], ident16[:, :], start=True, stop=True)
                last.then_inc(keys_turned, 1)

            pe.sem_inc(msgs_made, GPI)
            pe.sem_inc(back_made, GPI)
            pe.sem_inc(feats_turned, 2)
            pe.sem_inc(prods_made, 2)
            pe.sem_inc(root_prods_made, 2)
            pe.sem_inc(hot_used, 1)
            pe.sem_inc(wins_made, 2)
            pe.sem_inc(dense_made, SLABS)
            pe.wait_ge(first_weights_in, 16 * 3)
            pe.wait_ge(pool_const, 2)
            node_pass(0, with_keys=True)
            pe.wait_ge(weights_in, 16 * W_DMAS)
            nc.tensor.matmul(ps_deg[:, 0:NT], zbf[:, :], zbf[:, 0:NT], start=True, stop=False)
            edge_loop_slabs(0)
            nc.tensor.matmul(ps_deg[:, 0:NT], zbf[:, :], zbf[:, 0:NT], start=False, stop=True).then_inc(deg_made, 1)
            pe.wait_ge(deg_copied, 1)
            nc.tensor.matmul(ps_cum[:, 0:NT], tri[:, :], deg[:, :], start=True, stop=True)
            nc.tensor.matmul(ps_cum[:, NT:2 * NT], ones[:, :], deg[:, :], start=True, stop=True).then_inc(cum_made, 1)
            node_pass(1, with_keys=True)
            pe.wait_ge(bad_made, 1)
            nc.tensor.matmul(ps_cum[0:1, 0:1], ones[:, 0:1], bad[:, 0:1], start=True, stop=True).then_inc(bad_summed, 1)
            edge_loop_slabs(1)
            pe.wait_ge(ok_known, 1)
            ok = pe.value_load(ok_i[0:1, 0:1])
            with pe.If(ok):
                node_pass(2)
                dense_pass(3)
                dense_half(0, 1, 0, 2)
                dense_half(0, 1, 1)
                with pe.Fori(1, NTURNS - 1) as i:
                    for h in range(2):
                        dense_half(i, 1, h)
                for h in range(2):
                    dense_half(NTURNS - 1, 1, h, last=True)
            with pe.Else():
                for c in (2, 3):
                    node_pass(c)
                    edge_loop(c)

        @block.vector
        def _(dve):
            steps = [0]

            def link(ins):
                ins.then_inc(dve_step, 1)
                steps[0] += 1
                dve.wait_ge(dve_step, steps[0])

            def bcast(v):
                return v.rearrange("p (t a) -> p t a", a=1).to_broadcast([P, H, D])

            def turns(per):
                base = steps[0]
                with dve.Fori(0, NTURNS) as i:
                    seen = [0]

                    def hop(ins):
                        ins.then_inc(dve_step, 1)
                        seen[0] += 1
                        dve.wait_ge(dve_step, i * (2 * per) + (base + seen[0]))

                    yield i, hop
                    assert seen[0] == 2 * per, seen[0]
                steps[0] = base + 2 * per * NTURNS

            def add_parts(i, p, h):
                for s in range(h * H, (h + 1) * H):
                    dve.wait_ge(dense_made, i * B + ((p - 3) * NT + s) + (SLABS + 1))
                    nc.vector.tensor_reduce(
                        agg[:, s, :], ps_win[s % 2][:, 0:PARTS * D].rearrange("p (j d) -> p d j", j=PARTS),
                        AX.X, ALU.add).then_inc(dense_used, 1)

            def sums(i, p, h, hop, dense):
                hb = slice(h * H, (h + 1) * H)
                th = ds(i * B + h * H, H)
                dve.wait_ge(roots_made, half_no(i, p, h) - (HALVES - 3))
                if dense:
                    add_parts(i, p, h)
                    dve.wait_ge(dense_used, i * B + ((p - 3) * NT + h * H + H + 2))
                else:
                    dve.wait_ge(agg_in[h], (i + (p - 1) * NTURNS + 1) * (16 * H))
                if p in (3, 4):
                    hop(nc.vector.tensor_tensor(cent[:, :, :], agg[:, hb, :], bcast(inv_deg[:, th]), ALU.mult))
                    hop(nc.vector.tensor_tensor(tmp[:, :, :], cent[:, :, :], root[:, th, :], ALU.add))
                else:
                    hop(nc.vector.tensor_tensor(tmp[:, :, :], agg[:, hb, :], root[:, th, :], ALU.add))
                if not dense:
                    dve.sem_inc(agg_used, 1)

            def norm(i, p, h, hop):
                k = half_no(i, p // 2, h)
                dve.sem_inc(dve_passed, 1)
                for s in range(H):
                    last = nc.vector.bn_stats(stats[:, s, :], xs[:, ds(i * B + (h * H + s), 1), :].rearrange("p t d -> p (t d)"))
                hop(last)
                dve.sem_inc(dve_passed, 1)
                for s in range(H):
                    last = nc.vector.bn_aggr(mv[:, h, s, :], stats[:, s, :])
                last.then_inc(var_made, 1)
                dve.wait_ge(std_made, k + 1)
                hop(nc.vector.reciprocal(rstd[:, h, :], std[:, h, :]))
                nc.vector.scalar_tensor_tensor(shift[:, h, :], mv[:, h, :, 0], -1.0, rstd[:, h, :],
                                               ALU.mult, ALU.mult).then_inc(norm_made, 1)

            def node_half(i, h, p, hop, dense):
                th = ds(i * B + h * H, H)
                f = feat[:, h * H:(h + 1) * H, 0:D]
                xt = xs[:, th, :]
                sums(i, p, h, hop, dense)
                if p in (1, 3):
                    dve.wait_ge(feats_turned, half_no(i, p, h) + 1)
                if p == 1:
                    nc.vector.scalar_tensor_tensor(f, tmp[:, :, :], 0.01, tmp[:, :, :], ALU.mult, ALU.max).then_inc(feats_made, 1)
                if p == 3:
                    nc.vector.tensor_scalar(f, tmp[:, :, :], 0.0, None, ALU.max).then_inc(feats_made, 1)
                if p in (1, 3):
                    dve.wait_ge(feats_made, half_no(i, p, h) + 1)
                if p == 2:
                    hop(nc.vector.scalar_tensor_tensor(tmp[:, :, :], tmp[:, :, :], 0.01, tmp[:, :, :], ALU.mult, ALU.max))
                    hop(nc.vector.tensor_tensor(xt, xt, tmp[:, :, :], ALU.add))
                    norm(i, p, h, hop)
                if p == 4:
                    nc.vector.tensor_tensor(xt, xt, tmp[:, :, :], ALU.add).then_inc(out_made, 1)

            def node_pass(p, dense):
                for i, hop in turns({1: 1, 2: 5, 3: 2, 4: 2}[p]):
                    for h in range(2):
                        node_half(i, h, p, hop, dense)

            def split_kept():
                def rest(i):
                    t = ds(i * B, B)
                    part = [hparts[0][:, t, j * D:(j + 1) * D] for j in range(PARTS)]
                    nc.vector.tensor_copy(part[1], kept[:, t, :]).then_inc(kept_part2, 1)
                    dve.wait_ge(kept_part2, i + 1)
                    nc.vector.tensor_tensor(part[2], kept[:, t, :], part[1], ALU.subtract).then_inc(parts_made, 1)

                with dve.Fori(0, NTURNS - 1) as i:
                    dve.wait_ge(kept_less, i + 1)
                    rest(i)
                t = slice((NTURNS - 1) * B, NT)
                dve.wait_ge(prods_taken, 3 * HALVES + 2)
                link(nc.vector.tensor_tensor(kept[:, t, :], kept[:, t, :], hparts[0][:, t, 0:D], ALU.subtract))
                rest(NTURNS - 1)

            def edge_turn(i, c, quarter=None):
                if c == 0:
                    K = GPI * CPG
                    dve.wait_ge(hot_used, i + 1)
                    nc.vector.tensor_tensor(
                        hot_lo[:, :, :],
                        lo_b[:, ds(i * K, K)].rearrange("p (k a) -> p k a", a=1).to_broadcast([P, K, P]),
                        iota_b[:, :].rearrange("p (a m) -> p a m", a=1).to_broadcast([P, K, P]), ALU.is_equal)
                    nc.vector.tensor_tensor(
                        hot_hi[:, :, :],
                        hi_b[:, ds(i * K, K)].rearrange("p (k a) -> p k a", a=1).to_broadcast([P, K, NT]),
                        iota_b[:, 0:NT].rearrange("p (a m) -> p a m", a=1).to_broadcast([P, K, NT]),
                        ALU.is_equal).then_inc(hot_made, 1)
                for g in range(GPI):
                    n = group_no(i, c, g)
                    if quarter is not None:
                        v = i - 1
                        dve.wait_ge(wins_made, win_no(v, c, g) + 1)
                        for r in range(WCH):
                            col = v * (GPI * WCH) + (g * WCH + r + c * (CSLABS * 4 * GPI - KB_STEP * P) * WCH)
                            nc.vector.tensor_scalar(win_lo[:, g % 2, r, :], iota_k[:, 0:P], loT[:, ds(col, 1)],
                                                    None, ALU.is_equal)
                            last = nc.vector.tensor_scalar(win_key[:, g % 2, r, :], iota_k[:, 1:],
                                                           keyT[:, ds(col, 1)], None, ALU.is_equal)
                        last.then_inc(wins_hot, 1)
                    dve.wait_ge(mask_in[g], (i + c * TURNS + 1) * 16)
                    dve.wait_ge(msgs_made, n + GPI + 1)
                    dve.wait_ge(back_made, n + 1)
                    dve.wait_ge(scan_done, n + GPI)
                    nc.vector.tensor_tensor_scan(
                        scan[:, g, :], mask[:, g, :], ps_msg[g % 2][0:D, :], scan[:, (g - 1) % GPI, GROUP - 1:GROUP],
                        ALU.add if c in MAXC else ALU.mult,
                        ALU.max if c in MAXC else ALU.add).then_inc(scan_done, 1)

            def edge_loop(c):
                with dve.Fori(0, TURNS) as i:
                    edge_turn(i, c)

            def edge_loop_slabs(c):
                edge_turn(0, c)
                with dve.Fori(0, CSLABS) as j:
                    for quarter in range(4):
                        edge_turn(j * 4 + (quarter + 1), c, quarter)

            def keys(c, b):
                u = c * KB + b
                s_part, d_part = krow[:, b, :, 0:CHUNK], krow[:, b, :, CHUNK:2 * CHUNK]
                first = win_node[:, c * KB_STEP + b:c * KB_STEP + b + 1]
                dve.wait_ge(krow_in[b], 16 * WCH * (c + 1))
                nc.vector.tensor_tensor(k_loc[:, :, :], d_part,
                                        first.rearrange("p (a c) -> p a c", a=1).to_broadcast([P, WCH, CHUNK]), ALU.subtract)
                link(nc.vector.tensor_scalar(k_s[:, :, :], s_part, 7, 3, ALU.logical_shift_right, ALU.logical_shift_left))
                if u >= 1:
                    dve.wait_ge(keys_turned, u)
                link(nc.vector.scalar_tensor_tensor(k_key[:, :, :], k_s[:, :, :], 1.0, k_loc[:, :, :], ALU.add, ALU.add))
                link(nc.vector.tensor_scalar(k_loc[:, :, :], k_loc[:, :, :], -WIN, None, ALU.bitwise_and))
                nc.vector.scalar_tensor_tensor(k_key[:, :, :], k_loc[:, :, :], 0.0, k_key[:, :, :], ALU.is_equal, ALU.mult)
                link(nc.vector.scalar_tensor_tensor(k_lo[:, :, :], k_s[:, :, :], -float(P // WIN), s_part, ALU.mult, ALU.add))
                dve.sem_inc(krow_used, 1)
                dve.sem_inc(keys_made, 1)

            def make_keys(c):
                for b in range(KB):
                    keys(c, b)
                dve.wait_ge(keys_copied, (c + 1) * KB)

            dve.sem_inc(scan_done, GPI)
            dve.sem_inc(featT_copied, 2)
            dve.sem_inc(agg_used, 2)
            dve.sem_inc(back_copied, 2)
            dve.sem_inc(prods_taken, 2)
            dve.sem_inc(roots_made, 2)
            dve.sem_inc(wins_copied, 2)
            dve.sem_inc(dense_used, 2)
            dve.wait_ge(lines_in, 16)
            this, before, scratch = line[:, 1:], line[:, 0:CHUNKS], scratch_i[:, :].bitcast(fp32)
            link(nc.vector.tensor_tensor(scratch, this, before, ALU.not_equal))
            nc.vector.tensor_scalar(mask_max[:, :], scratch, -BIG, None, ALU.mult)
            nc.vector.tensor_scalar(mask_sum[:, :], scratch, -1.0, 1.0, ALU.mult, ALU.add).then_inc(masks_made, 1)
            dve.wait_ge(masks_made, 1)
            link(nc.vector.tensor_scalar(scratch_i[:, :], this, 7, None, ALU.logical_shift_right))
            nc.vector.tensor_copy(hi_b[:, :], scratch_i[:, :])
            link(nc.vector.tensor_scalar(this, this, P - 1, None, ALU.bitwise_and))
            nc.vector.tensor_copy(lo_b[:, :], this)
            dve.wait_ge(nodes_in, 32)
            dve.wait_ge(pool_const, 2)
            nc.vector.tensor_copy(ident16[:, :], ident[:, :])
            nc.vector.tensor_copy(iota_k[:, :], iota_i)
            link(nc.vector.tensor_copy(win_node_f[:, :], win_node[:, :]))
            for t in range(NTURNS):
                for h in range(2):
                    norm(t, 0, h, link)
                    b = 2 * t + h - 1
                    if b == 0:
                        dve.wait_ge(rows_in, 16)
                        link(nc.vector.tensor_copy(row_first[:, :], row_i))
                    if 0 <= b < WB:
                        link(nc.vector.tensor_scalar(row_flag[:, :], row_first[:, :], win_node_f[:, b:b + 1], 0.0, ALU.is_lt, ALU.add,
                                                     accum_out=row_at[:, 0, b:b + 1]))
                    if b == WB:
                        link(nc.vector.tensor_scalar(row_at[:, 0, :], row_at[:, 0, :], -1.0, 0.0, ALU.add, ALU.max))
                        for r in range(WCH):
                            link(nc.vector.tensor_scalar(row_idx[:, :, r], row_at[:, 0, :], float(r), None, ALU.add))
                        dve.sem_inc(rows_known, 1)
            link(nc.vector.tensor_copy(iota_b[:, :], iota_i[:, 0:P]))
            make_keys(0)
            edge_loop_slabs(0)

            tot, pre, endf, nonzero = (cnt[k] for k in ("tot", "pre", "endf", "nonzero"))
            dve.wait_ge(deg_made, 1)
            nc.vector.tensor_copy(deg[:, :], ps_deg[:, 0:NT]).then_inc(deg_copied, 1)
            dve.wait_ge(cum_made, 1)
            link(nc.vector.tensor_copy(tot[:, :], ps_cum[:, NT:2 * NT]))
            link(nc.vector.tensor_tensor_scan(pre[:, :], ones[:, 0:NT], tot[:, :], 0.0, ALU.mult, ALU.add))
            link(nc.vector.tensor_tensor(pre[:, :], pre[:, :], tot[:, :], ALU.subtract))
            link(nc.vector.tensor_tensor(endf[:, :], ps_cum[:, 0:NT], pre[:, :], ALU.add))
            link(nc.vector.tensor_scalar(endf[:, :], endf[:, :], -1.0, 0.0, ALU.add, ALU.max))
            link(nc.vector.tensor_copy(end_i[:, :], endf[:, :]))
            link(nc.vector.tensor_scalar(part[:, :], end_i[:, :], 9, 9, ALU.logical_shift_right, ALU.logical_shift_left))
            link(nc.vector.tensor_scalar(part2[:, :], end_i[:, :], P - 1, 2, ALU.bitwise_and, ALU.logical_shift_left))
            link(nc.vector.tensor_tensor(part[:, :], part[:, :], part2[:, :], ALU.bitwise_or))
            link(nc.vector.tensor_scalar(part2[:, :], end_i[:, :], 7, CPG - 1, ALU.logical_shift_right, ALU.bitwise_and))
            link(nc.vector.tensor_tensor(part[:, :], part[:, :], part2[:, :], ALU.bitwise_or))
            link(nc.vector.tensor_scalar(nonzero[:, :], deg[:, :], 0.0, None, ALU.is_gt))
            link(nc.vector.tensor_scalar(endf[:, :], part[:, :], -float(ZROW), None, ALU.add))
            link(nc.vector.tensor_tensor(endf[:, :], endf[:, :], nonzero[:, :], ALU.mult))
            link(nc.vector.tensor_scalar(end_row[:, :], endf[:, :], float(ZROW), None, ALU.add))
            dve.sem_inc(end_rows_made, 1)
            link(nc.vector.tensor_scalar(inv_deg[:, :], deg[:, :], 1.0, None, ALU.max))
            link(nc.vector.reciprocal(inv_deg[:, :], inv_deg[:, :]))
            dve.wait_ge(nexts_in, 32)
            link(nc.vector.tensor_tensor(bad_w[:, :], row_at[:, 1, :], row_at[:, 0, :], ALU.subtract))
            link(nc.vector.tensor_scalar(bad_w[:, :], bad_w[:, :], float(WCH - 1), None, ALU.is_gt))
            link(nc.vector.tensor_scalar(bad_d[:, :], deg[:, 0:HI], float(DEG_CAP), None, ALU.is_gt))
            dve.sem_inc(rows_known, 1)
            node_pass(1, False)
            dve.wait_ge(rows_known, 3)
            link(nc.vector.reduce_sum(bad[:, 0:1], bad_w[:, :], AX.X))
            link(nc.vector.reduce_sum(bad[:, 1:2], bad_d[:, :], AX.X))
            link(nc.vector.tensor_tensor(bad[:, 0:1], bad[:, 0:1], bad[:, 1:2], ALU.add))
            dve.sem_inc(bad_made, 1)
            make_keys(1)
            dve.wait_ge(bad_summed, 1)
            nc.vector.tensor_scalar(ok_i[:, :], ps_cum[0:1, 0:1], 0.0, None, ALU.is_equal).then_inc(ok_known, 1)
            edge_loop_slabs(1)
            ok = dve.value_load(ok_i[0:1, 0:1])
            at = steps[0]
            with dve.If(ok):
                node_pass(2, False)
                split_kept()
                node_pass(3, True)
                node_pass(4, True)
            with dve.Else():
                steps[0] = at
                node_pass(2, False)
                edge_loop(2)
                node_pass(3, False)
                edge_loop(3)
                node_pass(4, False)


_INS = ["x", "src_t", "dst_t", "dst_line", "edges_packed", "attr_t",
        "L0_gnn_W1_msg", "L0_gnn_W1_edge", "L0_gnn_W1_root", "L0_gnn_b1",
        "L0_gnn_W2_msg", "L0_gnn_W2_edge", "L0_gnn_W2_root", "L0_gnn_b2",
        "L1_gnn_W_self1", "L1_gnn_W_neigh1", "L1_gnn_b1",
        "L1_gnn_W_self2", "L1_gnn_W_neigh2", "L1_gnn_b2"]


def kernel(**inputs):
    import numpy as np
    import concourse.bacc as _bacc
    from concourse import mybir as _mybir
    from concourse.bass_utils import run_bass_kernel_spmd as _run

    a = {k: np.asarray(v) for k, v in inputs.items()}
    src = np.concatenate([a["src"], np.zeros(EP - E, a["src"].dtype)])
    dst = np.concatenate([a["dst"], np.full(EP - E, PADN, a["dst"].dtype)])
    a["src_t"] = src.reshape(CHUNKS, P).T
    a["dst_t"] = dst.reshape(CHUNKS, P).T
    line = np.concatenate([np.full(1, -1, dst.dtype), dst])
    a["dst_line"] = np.stack([line[p * CHUNKS:(p + 1) * CHUNKS + 1] for p in range(P)])
    more = WCH * CHUNK
    both = [np.concatenate([v, np.full(more, PADN, v.dtype)]).reshape(EROWS, CHUNK) for v in (src, dst)]
    a["edges_packed"] = np.concatenate(both, axis=1)
    attr = np.concatenate([a["edge_attr_32"], np.zeros((EP - E, DA), a["edge_attr_32"].dtype)])
    a["attr_t"] = attr.reshape(TURNS, GPI, GROUP, DA).transpose(0, 1, 3, 2).reshape(TURNS * P, GROUP)

    nc = _bacc.Bacc("TRN2", target_bir_lowering=False, num_devices=1)
    arrays, args = {}, []
    for name in _INS:
        v = np.ascontiguousarray(a[name])
        arrays[f"in_{name}_dram"] = v
        args.append(nc.dram_tensor(f"in_{name}_dram", v.shape, _mybir.dt.from_np(v.dtype), kind="ExternalInput").ap())
    args.append(nc.dram_tensor("out_0_dram", (N, D), _mybir.dt.float32, kind="ExternalOutput").ap())
    gnn_kernel(nc, *args)
    r = _run(nc, [arrays], core_ids=[0])
    return r.results[0]["out_0_dram"]
```
